# Optimizing a Trainium2 kernel written in Bass

```python
import numpy as np
import jax
import jax.numpy as jnp

def _softmax(x, axis=-1):
    return jax.nn.softmax(x, axis=axis)

def _gelu(x):
    return jax.nn.gelu(x, approximate=True)

def _silu(x):
    return jax.nn.silu(x)

def _sigmoid(x):
    return jax.nn.sigmoid(x)

def _layernorm(x, axis=-1, eps=1e-05):
    m = jnp.mean(x, axis=axis, keepdims=True)
    v = jnp.var(x, axis=axis, keepdims=True)
    return (x - m) / jnp.sqrt(v + eps)

def _scatter_add(tgt, idx, src, axis=0):
    return tgt.at[idx].add(src)

def _segment_sum(src, seg, n):
    return jax.ops.segment_sum(src, seg, n)
kernel_name = 'mk_adaln_d1_jaxref_r4_04afa4'

def setup_inputs(seed: int=0):
    np.random.seed(seed)
    _w = jnp.asarray

    def _L0_attn_setup():
        import jax, jax.numpy as jnp
        import numpy as np
        EMBED_DIM = 512
        NUM_HEADS = 16
        BLOCK_SIZE = 128

        def _flash_attention_v2(q, k, v, block_size, scale):
            B, H, S, D = q.shape
            nb = S // block_size
            qb = q.reshape(B, H, nb, block_size, D)
            kb = k.reshape(B, H, nb, block_size, D).transpose(2, 0, 1, 3, 4)
            vb = v.reshape(B, H, nb, block_size, D).transpose(2, 0, 1, 3, 4)
            out0 = jnp.zeros_like(qb)
            l0 = jnp.zeros((B, H, nb, block_size, 1), dtype=q.dtype)
            m0 = jnp.full((B, H, nb, block_size, 1), -jnp.inf, dtype=q.dtype)

            def step(carry, kv):
                out, l, m = carry
                k_j, v_j = kv
                s = jnp.einsum('bhnqd,bhkd->bhnqk', qb, k_j) * scale
                m_ij = jnp.max(s, axis=-1, keepdims=True)
                p = jnp.exp(s - m_ij)
                l_ij = jnp.sum(p, axis=-1, keepdims=True)
                m_new = jnp.maximum(m, m_ij)
                alpha = jnp.exp(m - m_new)
                beta = jnp.exp(m_ij - m_new)
                l_new = alpha * l + beta * l_ij
                pv = jnp.einsum('bhnqk,bhkd->bhnqd', p, v_j)
                out_new = alpha * l / l_new * out + beta * l_ij / l_new * pv
                return ((out_new, l_new, m_new), None)
            (out, _, _), _ = jax.lax.scan(step, (out0, l0, m0), (kb, vb))
            return out.reshape(B, H, S, D)
        key = jax.random.key(seed)
        k1, k2, k3 = jax.random.split(key, 3)
        B, S, E = (2, 1024, EMBED_DIM)
        x = jax.random.normal(k1, (B, S, E), dtype=jnp.float32)
        w_qkv = jax.random.normal(k2, (3 * E, E), dtype=jnp.float32) * 0.02
        w_out = jax.random.normal(k3, (E, E), dtype=jnp.float32) * 0.02
        b_out = jnp.zeros((E,), dtype=jnp.float32)
        return {'x': x, 'w_qkv': w_qkv, 'w_out': w_out, 'b_out': b_out}
    _L0_attn_in = _L0_attn_setup()

    def _L0_ffn_setup():
        import jax, jax.numpy as jnp
        import numpy as np
        TOPK = 2
        NORM_TOPK = True
        SCALE = 1.0
        EPS = 1e-09
        key = jax.random.key(seed)
        ks = jax.random.split(key, 9)
        h, i, E = (512, 256, 16)
        std = 0.02
        return {'x': jax.random.normal(ks[0], (1, 512, h), jnp.float32), 'Wr': jax.random.normal(ks[1], (E, h), jnp.float32) * std, 'bias': jnp.zeros((E,), jnp.float32), 'Wg': jax.random.normal(ks[2], (E, h, i), jnp.float32) * std, 'Wu': jax.random.normal(ks[3], (E, h, i), jnp.float32) * std, 'Wd': jax.random.normal(ks[4], (E, i, h), jnp.float32) * std, 'sWg': jax.random.normal(ks[5], (h, i), jnp.float32) * std, 'sWu': jax.random.normal(ks[6], (h, i), jnp.float32) * std, 'sWd': jax.random.normal(ks[7], (i, h), jnp.float32) * std}
    _L0_ffn_in = _L0_ffn_setup()
    _L0_c = _w((lambda *s: np.random.randn(*s).astype(np.float32) * 0.05)(8, 512))
    _L0_wmod = _w((lambda *s: np.random.randn(*s).astype(np.float32) * 0.05)(512, 6 * 512) * 512 ** (-0.5))
    _d = {'L0_attn_x': _L0_attn_in['x'], 'L0_attn_w_qkv': _L0_attn_in['w_qkv'], 'L0_attn_w_out': _L0_attn_in['w_out'], 'L0_attn_b_out': _L0_attn_in['b_out'], 'L0_ffn_Wr': _L0_ffn_in['Wr'], 'L0_ffn_bias': _L0_ffn_in['bias'], 'L0_ffn_Wg': _L0_ffn_in['Wg'], 'L0_ffn_Wu': _L0_ffn_in['Wu'], 'L0_ffn_Wd': _L0_ffn_in['Wd'], 'L0_ffn_sWg': _L0_ffn_in['sWg'], 'L0_ffn_sWu': _L0_ffn_in['sWu'], 'L0_ffn_sWd': _L0_ffn_in['sWd'], 'L0_c': _L0_c, 'L0_wmod': _L0_wmod}
    _x0 = _d['L0_attn_x']
    _d['L0_attn_x'] = jax.random.normal(jax.random.fold_in(jax.random.key(seed), 1), (8, 512, 512), dtype=_x0.dtype)
    del _x0
    return _d

def reference(L0_attn_x, L0_attn_w_qkv, L0_attn_w_out, L0_attn_b_out, L0_ffn_Wr, L0_ffn_bias, L0_ffn_Wg, L0_ffn_Wu, L0_ffn_Wd, L0_ffn_sWg, L0_ffn_sWu, L0_ffn_sWd, L0_c, L0_wmod):

    def _L0_attn_ref(x, w_qkv, w_out, b_out):
        import jax, jax.numpy as jnp
        import numpy as np
        EMBED_DIM = 512
        NUM_HEADS = 16
        BLOCK_SIZE = 128

        def _flash_attention_v2(q, k, v, block_size, scale):
            B, H, S, D = q.shape
            nb = S // block_size
            qb = q.reshape(B, H, nb, block_size, D)
            kb = k.reshape(B, H, nb, block_size, D).transpose(2, 0, 1, 3, 4)
            vb = v.reshape(B, H, nb, block_size, D).transpose(2, 0, 1, 3, 4)
            out0 = jnp.zeros_like(qb)
            l0 = jnp.zeros((B, H, nb, block_size, 1), dtype=q.dtype)
            m0 = jnp.full((B, H, nb, block_size, 1), -jnp.inf, dtype=q.dtype)

            def step(carry, kv):
                out, l, m = carry
                k_j, v_j = kv
                s = jnp.einsum('bhnqd,bhkd->bhnqk', qb, k_j) * scale
                m_ij = jnp.max(s, axis=-1, keepdims=True)
                p = jnp.exp(s - m_ij)
                l_ij = jnp.sum(p, axis=-1, keepdims=True)
                m_new = jnp.maximum(m, m_ij)
                alpha = jnp.exp(m - m_new)
                beta = jnp.exp(m_ij - m_new)
                l_new = alpha * l + beta * l_ij
                pv = jnp.einsum('bhnqk,bhkd->bhnqd', p, v_j)
                out_new = alpha * l / l_new * out + beta * l_ij / l_new * pv
                return ((out_new, l_new, m_new), None)
            (out, _, _), _ = jax.lax.scan(step, (out0, l0, m0), (kb, vb))
            return out.reshape(B, H, S, D)
        B, S, E = x.shape
        H = NUM_HEADS
        D = E // H
        scale = 1.0 / np.sqrt(D).astype(np.float32)
        qkv = (x @ w_qkv.T).reshape(B, S, 3, H, D)
        q, k, v = jnp.moveaxis(qkv, 2, 0)
        q = q.transpose(0, 2, 1, 3)
        k = k.transpose(0, 2, 1, 3)
        v = v.transpose(0, 2, 1, 3)
        out = _flash_attention_v2(q, k, v, BLOCK_SIZE, scale)
        out = out.transpose(0, 2, 1, 3).reshape(B, S, E)
        return out @ w_out.T + b_out

    def _L0_ffn_ref(x, Wr, bias, Wg, Wu, Wd, sWg, sWu, sWd):
        import jax, jax.numpy as jnp
        import numpy as np
        TOPK = 2
        NORM_TOPK = True
        SCALE = 1.0
        EPS = 1e-09
        b, s, h = x.shape
        E = Wr.shape[0]
        xt = x.reshape(b * s, h)
        logits = xt @ Wr.T + bias
        probs = jax.nn.softmax(logits, axis=-1)
        topk_val, topk_idx = jax.lax.top_k(probs, TOPK)
        if NORM_TOPK:
            w = topk_val / (jnp.sum(topk_val, axis=-1, keepdims=True) + EPS)
        else:
            w = topk_val
        w = w * SCALE
        g = jnp.einsum('th,ehi->tei', xt, Wg)
        u = jnp.einsum('th,ehi->tei', xt, Wu)
        y = jnp.einsum('tei,eih->teh', jax.nn.silu(g) * u, Wd)
        oh = jax.nn.one_hot(topk_idx, E, dtype=x.dtype)
        routed = jnp.einsum('tke,tk,teh->th', oh, w, y)
        shared = jax.nn.silu(xt @ sWg) * (xt @ sWu) @ sWd
        return (routed + shared).reshape(b, s, h)
    x = L0_attn_x
    mod = (_silu(L0_c) @ L0_wmod).reshape(L0_c.shape[0], 6, 1, -1)
    sa, ca, ga, sb, cb, gb = (mod[:, 0], mod[:, 1], mod[:, 2], mod[:, 3], mod[:, 4], mod[:, 5])
    ga = (2 * (ga >= 0) - 1) * jnp.maximum(jnp.abs(ga), 0.25)
    gb = (2 * (gb >= 0) - 1) * jnp.maximum(jnp.abs(gb), 0.25)
    h = _layernorm(x, axis=-1) * (1 + ca) + sa
    x = x + ga * _L0_attn_ref(h, L0_attn_w_qkv, L0_attn_w_out, L0_attn_b_out)
    h = _layernorm(x, axis=-1) * (1 + cb) + sb
    x = x + gb * _L0_ffn_ref(h, L0_ffn_Wr, L0_ffn_bias, L0_ffn_Wg, L0_ffn_Wu, L0_ffn_Wd, L0_ffn_sWg, L0_ffn_sWu, L0_ffn_sWd)
    return x

_drawn_inputs = setup_inputs


def setup_inputs(seed=0):
    import zlib

    import numpy as np

    out = dict(_drawn_inputs(seed))
    spreads = {'L0_attn_b_out': (0.0, 0.342), 'L0_ffn_bias': (0.0, 0.8)}
    factors = {'L0_ffn_Wr': 8.0,
     'L0_ffn_Wg': 8.0,
     'L0_ffn_Wu': 8.0,
     'L0_ffn_Wd': 8.0,
     'L0_ffn_sWg': 6.753,
     'L0_ffn_sWu': 6.577,
     'L0_ffn_sWd': 6.596}
    for name, (base, spread) in spreads.items():
        noise = np.random.default_rng([zlib.crc32(name.encode()), seed]).standard_normal(out[name].shape)
        drawn = base * np.exp(spread * noise) if base else spread * noise
        out[name] = jnp.asarray(drawn.astype(out[name].dtype))
    for name, factor in factors.items():
        out[name] = (out[name] * factor).astype(out[name].dtype)
    return out
```

```python
import concourse.bass as bass
from concourse import mybir
from contextlib import ExitStack


def adaln_moe_block_kernel(nc, x, wqkvT, woutT, b_out, wrT, r_bias, Wg, Wu, Wd, sWg, sWu, sWd, cT, wmod, out):
    f32 = mybir.dt.float32
    f32r = mybir.dt.float32r
    i32 = mybir.dt.int32
    ALU = mybir.AluOpType
    ACT = mybir.ActivationFunctionType
    AX = mybir.AxisListType

    NB, SEQ, D = x.shape
    P = 128
    KT = D // P
    TT = SEQ // P
    NT = NB * TT
    H = 16
    HD = D // H
    HG = P // HD
    NG = H // HG
    SCALE = 1.0 / float(HD) ** 0.5
    EPS = 1e-5
    NE = Wg.shape[0]
    FI = Wg.shape[2]
    MI = FI // P
    U = NG * TT * HG
    UG = TT * HG
    GA, GAB, CB1, SB, GB = range(5)
    NMOD = 5

    NST = 2 * NT + NE
    WSLOTS = 4
    WLEN = KT * 2 * FI + MI * D

    mod_d = nc.dram_tensor("mod_rows", (NMOD, NB, D), f32).ap()
    x1_d = nc.dram_tensor("x1_rows", (NT, P, D), f32).ap()
    h2_d = nc.dram_tensor("h2_rows", (NT * P, D), f32).ap()
    h2T_d = nc.dram_tensor("h2_transposed", (NB, TT, P, KT * P), f32).ap()
    y_d = nc.dram_tensor("routed_rows", (NST * P, D), f32).ap()

    x_t = x.rearrange("b (t p) d -> b p t d", p=P)
    x_tile = x.rearrange("b (t p) d -> (b t) p d", p=P)
    out_tile = out.rearrange("b (t p) d -> (b t) p d", p=P)
    wqkv_v = wqkvT.rearrange("(k p) n -> p k n", p=P)
    wout_v = woutT.rearrange("(k p) n -> p k n", p=P)
    wr_v = wrT.rearrange("(k p) n -> p k n", p=P)
    wmod_v = wmod.rearrange("(k p) n -> p k n", p=P)
    cT_v = cT.rearrange("(k p) n -> p k n", p=P)
    Wg_v = Wg.rearrange("e (k p) i -> e p k i", p=P)
    Wu_v = Wu.rearrange("e (k p) i -> e p k i", p=P)
    Wd_v = Wd.rearrange("e (m p) d -> e p m d", p=P)

    BODY = [(3, "v", 0), (4, "v", 1), (5, "v", 2), (6, "v", 3),
            (8, "q", 1), (10, "k", 1),
            (12, "out", 0), (14, "out", 1), (16, "out", 2), (18, "out", 3),
            (22, "q", 2), (25, "k", 2),
            (28, "tr", 0), (30, "tr", 1), (31, "route", 0), (33, "tr", 2), (34, "route", 1),
            (35, "tr", 3), (36, "route", 2), (37, "route", 3),
            (39, "q", 3), (42, "k", 3),
            (46, "ht", 0), (47, "ht", 1), (48, "ht", 2), (49, "ht", 3),
            (53, "q", 0), (57, "k", 0)]
    TAIL = ([(5 + 3 * t, "out", t) for t in range(TT)]
            + [w for t in range(TT) for w in ((19 + 2 * t, "tr", t), (20 + 2 * t, "route", t))])
    TAIL_END = 30
    OF_PREV = ("out", "tr", "route")

    def of_next(kind, i):
        return kind == "ht" or (kind in "qk" and i == 0)

    def runs(kind, i, b):
        return b is None or not ((b == 0 and kind in OF_PREV) or (b == NB - 1 and of_next(kind, i)))

    PRO = [("modT", 0)] + [("ht", k) for k in range(KT)] + [("q", 0), ("k", 0)] + [("mod", m) for m in range(4)]
    DBANKS = 3
    dense_order = [(-1, k, i) for k, i in PRO]
    for _b in range(NB):
        dense_order += [(_b, k, i) for _, k, i in BODY if runs(k, i, _b)]
    dense_order += [(NB, k, i) for _, k, i in TAIL]
    body_len = len(BODY)
    per_bank = [len(range(n, body_len, DBANKS)) for n in range(DBANKS)]
    place = {}
    used = [0] * DBANKS
    for _n, (_b, _k, _i) in enumerate(dense_order):
        if 0 <= _b < NB:
            bank = [n for n, (_, k, i) in enumerate(BODY) if (k, i) == (_k, _i)][0] % DBANKS
        else:
            bank = _n % DBANKS
        place[(_b, _k, _i)] = (bank, _n, used[bank])
        used[bank] += 1

    class Batch:

        def __init__(self, at, reg=None):
            self.at, self.reg = at, reg

        def lin(self, per, off):
            return per * self.reg + off if self.reg is not None else per * self.at + off

        def dense(self, kind, i):
            if self.reg is None:
                return place[(self.at, kind, i)]
            bank, n, uses = place[(1, kind, i)]
            return bank, self.lin(body_len, n - body_len), self.lin(per_bank[bank], uses - per_bank[bank])

        def has(self, kind, i):
            return runs(kind, i, None if self.reg is not None else self.at)

        @property
        def first(self):
            return self.reg is None and self.at == 0

        @property
        def after_last(self):
            return self.reg is None and self.at == NB

        def work(self, u, lag=0):
            table = TAIL if self.after_last else BODY
            return [(k, i) for at, k, i in table if at == u - lag and (self.after_last or self.has(k, i))]

    def wait(eng, sem, value):
        if not isinstance(value, int) or value > 0:
            eng.wait_ge(sem, value)

    LAG = 3
    AV_AT = LAG + HG

    def scaled_by_vector(c):
        return c % HG == 0

    def wait_scaled(eng, b, c, by_vector, by_pool):
        if scaled_by_vector(c):
            wait(eng, by_vector, b.lin(U // HG, c // HG + 1))
        else:
            wait(eng, by_pool, b.lin(U // HG * (HG - 1), c // HG * (HG - 1) + c % HG))

    def before(b, u, lag):
        return (u < lag or not b.after_last) and (u >= lag or not b.first)

    ctx = ExitStack()
    with ctx:
        def sb(name, shape, dt=f32):
            return ctx.enter_context(nc.sbuf_tensor(name, shape, dt))

        def sem(name):
            return ctx.enter_context(nc.semaphore(name))

        ps = ctx.enter_context(nc.psum_tensor("ps", [P, 8, 512], f32))
        S_BANK, PT_BANK, AV_BANK, D_BANK = 0, 2, 4, 5

        ident = sb("ident", [P, P])
        wr_hi = sb("wr_hi", [P, KT, NE], f32r)
        wr_lo = sb("wr_lo", [P, KT, NE], f32r)
        wr_raw = sb("wr_raw", [P, KT, NE])
        scT = sb("silu_c", [P, KT, NB])
        modT = sb("sa_ca_columns", [P, 2, KT, NB])
        rbias = sb("router_bias", [P, NE])
        logits = sb("logits", [P, NT, NE])

        one = ExitStack()

        def sb1(name, shape, dt=f32):
            return one.enter_context(nc.sbuf_tensor(name, shape, dt))

        wqkv_hi = sb1("wqkv_hi", [P, KT, 3 * D], f32r)
        wqkv_lo = sb1("wqkv_lo", [P, KT, 3 * D], f32r)
        wout_hi = sb1("wout_hi", [P, KT, D], f32r)
        wout_lo = sb1("wout_lo", [P, KT, D], f32r)
        hT_hi = sb1("hT_hi", [P, KT, SEQ], f32r)
        hT_lo = sb1("hT_lo", [P, KT, SEQ], f32r)
        ht_full = sb1("ht_full", [P, SEQ])
        xnat = sb1("xnat", [P, TT, D])
        half_hi = sb1("half_hi", [P, 2, SEQ], f32r)
        half_lo = sb1("half_lo", [P, 2, SEQ], f32r)
        qstack = sb1("qstack", [P, 2, HG, SEQ], f32r)
        kstack = sb1("kstack", [P, 2, HG, SEQ], f32r)
        V = sb1("V", [P, TT, D])
        probs = sb1("probs", [P, 4, SEQ])
        probsT = sb1("probsT", [P, HG, TT, P])
        neg_max = sb1("neg_max", [P, 4, TT])
        neg_top = sb1("neg_top", [P, 4])
        sums = sb1("sums", [P, 4, TT])
        weight = sb1("weight", [P, 4, TT])
        weighed = sb1("weighed", [P, 4, TT])
        total = sb1("total", [P, 4])
        factor = sb1("factor", [P, 4, TT])
        outT_hi = sb1("outT_hi", [P, NG, SEQ], f32r)
        outT_lo = sb1("outT_lo", [P, NG, SEQ], f32r)
        post = sb1("post", [P, 4, D])
        h2 = sb1("h2", [P, TT, D])
        h2T = sb1("h2T", [P, KT, P])
        h2T_hi = sb1("h2T_hi", [P, KT, P], f32r)
        h2T_lo = sb1("h2T_lo", [P, KT, P], f32r)
        bc = sb1("bc", [P, 4, D])
        stats1 = sb1("stats1", [P, TT, 6])
        mv1 = sb1("mv1", [P, TT, 2])
        rstd1 = sb1("rstd1", [P, TT])
        minus_half = sb1("minus_half", [P, TT])
        stats2 = sb1("stats2", [P, 2, 6])
        mv2 = sb1("mv2", [P, 2, 2])
        rstd2 = sb1("rstd2", [P, 2])

        one.close()

        base = sb("base", [P, NT, D])
        wslots = sb("wslots", [P, WSLOTS * WLEN])
        wts = sb("token_weights", [P, 2, NT])
        slot_i = sb("slot_i", [P, 2, NT], i32)
        gather_i = sb("gather_i", [P, NST], i32)
        need_i = sb("need_i", [1, NST], i32)
        woff_i = sb("woff_i", [1, NST], i32)
        freed_i = sb("freed_i", [1, NE], i32)
        three_ = ExitStack()

        def sb3(name, shape, dt=f32):
            return three_.enter_context(nc.sbuf_tensor(name, shape, dt))

        sgu_hi = sb3("sgu_hi", [P, KT, 2 * FI], f32r)
        sgu_lo = sb3("sgu_lo", [P, KT, 2 * FI], f32r)
        swd_hi = sb3("swd_hi", [P, MI, D], f32r)
        swd_lo = sb3("swd_lo", [P, MI, D], f32r)
        s_raw = sb3("s_raw", [P, TT, KT, P])
        s_hi = sb3("s_hi", [P, TT, KT, P], f32r)
        s_lo = sb3("s_lo", [P, TT, KT, P], f32r)
        s_gate = sb3("s_gate", [P, MI, SEQ])
        s_act = sb3("s_act", [P, MI, SEQ])
        a_hi = sb3("a_hi", [P, MI, SEQ], f32r)
        a_lo = sb3("a_lo", [P, MI, SEQ], f32r)
        gbrow = sb3("gbrow", [P, D])
        scaled = sb3("scaled", [P, 2, D])
        sgu_raw = base[:, NT - 8:NT - 4, :]
        swd_raw = base[:, NT - 4:NT - 4 + MI, :]

        r_at = [2 * WLEN]

        def rt(n, dt=f32):
            r_at[0] += n
            assert r_at[0] <= WSLOTS * WLEN
            v = wslots[:, r_at[0] - n:r_at[0]]
            return v if dt == f32 else v.bitcast(dt)

        TE = NT * NE
        prob = rt(TE)
        eq = rt(TE)
        order = rt(TE)
        oh = [rt(TE), rt(TE)]
        tot_e = rt(TE)
        run = rt(TE)
        slot_of = rt(TE)
        ones_te = rt(TE)
        iota_e = rt(NE)
        iota_t = rt(NST)
        row_max, row_sum = rt(NT), rt(NT)
        top = [rt(NT), rt(NT)]
        first = rt(NT)
        den = rt(NT)
        cnt = rt(NE)
        cum_prev = rt(NE)
        tiles_i = rt(NE, i32)
        tiles = rt(NE)
        tiles_cum = rt(NE)
        offset = rt(NE)
        slots = rt(2 * NT)
        slots_hi, slots_lo = rt(2 * NT), rt(2 * NT)
        tmp_i = rt(2 * NT, i32)
        tmp2_i = rt(2 * NT, i32)
        e_tab = rt(NST)
        e_tab_i = rt(NST, i32)
        tokid = rt(NT)
        tri = sb3("tri", [P, P], mybir.dt.bfloat16)
        ones_b = sb3("ones_b", [P, P], mybir.dt.bfloat16)
        mask = sb3("mask", [P, TE], mybir.dt.bfloat16)
        iota_p = sb3("iota_p", [P, P])
        hot_lo = sb3("hot_lo", [P, 2, P], f32r)
        hot_hi = sb3("hot_hi", [P, 2, NST], f32r)
        three_.close()

        four = ExitStack()

        def sb4(name, shape, dt=f32):
            return four.enter_context(nc.sbuf_tensor(name, shape, dt))

        RING = 4
        xg = sb4("xg", [P, RING, D])
        xT = sb4("xT", [P, 2, KT, P])
        gate = sb4("gate", [P, 2, FI])
        inner = sb4("inner", [P, 2, FI])
        innerT = sb4("innerT", [P, 2, MI, P])
        yrow = sb4("yrow", [P, RING, D])
        gidx = sb4("gidx", [P, RING], i32)
        four.close()
        five = ExitStack()
        rows0 = five.enter_context(nc.sbuf_tensor("rows0", [P, TT, D], f32))
        rows1 = five.enter_context(nc.sbuf_tensor("rows1", [P, TT, D], f32))
        gb2 = five.enter_context(nc.sbuf_tensor("gb2", [P, D], f32))
        ridx = five.enter_context(nc.sbuf_tensor("ridx", [P, 2, TT], i32))
        five.close()
        identity_ready = sem("identity_ready")
        const_in = sem("const_in")
        silu_c_ready = sem("silu_c_ready")
        chunk_in = [sem("chunk_in0"), sem("chunk_in1")]
        w_hi_done = sem("w_hi_done")
        w_lo_done = sem("w_lo_done")
        modT_done = sem("modT_done")
        row_step = sem("row_step")
        gate_step = sem("gate_step")
        row_out = sem("row_out")
        x_in = sem("x_in")
        ln1_step = sem("ln1_step")
        rstd1_step = sem("rstd1_step")
        xn_done = sem("xn_done")
        ht_hi_done = sem("ht_hi_done")
        ht_lo_done = sem("ht_lo_done")
        dense_ready = sem("dense_ready")
        dense_free = [sem(f"dense_free{n}") for n in range(DBANKS)]
        half_hi_done = sem("half_hi_done")
        q_stacked = sem("q_stacked")
        k_stacked = sem("k_stacked")
        scores_ready = sem("scores_ready")
        max_ready = sem("max_ready")
        exp_done = sem("exp_done")
        block_max_done = sem("block_max_done")
        weight_done = sem("weight_done")
        factor_step = sem("factor_step")
        scaled_v = sem("scaled_v")
        scaled_p = sem("scaled_p")
        pt_ready = sem("pt_ready")
        pt_free = [sem("pt_free0"), sem("pt_free1")]
        av_done = sem("av_done")
        av_free = sem("av_free")
        out_hi_done = sem("out_hi_done")
        bc_in = sem("bc_in")
        xr_in = [sem("xr_in0"), sem("xr_in1")]
        xb_done = sem("xb_done")
        x1_done = sem("x1_done")
        x1_out = [sem("x1_out0"), sem("x1_out1")]
        ln2_step = sem("ln2_step")
        rstd2_step = sem("rstd2_step")
        h2_normal = sem("h2_normal")
        h2_step = sem("h2_step")
        h2_out = sem("h2_out")
        tr_lo_done = sem("tr_lo_done")
        h2T_out = sem("h2T_out")
        phase_end = sem("phase_end")
        passed_pool = sem("passed_pool")
        passed_dve = sem("passed_dve")
        passed_sp = sem("passed_sp")

        def wait_apart(eng, sem, value, passed):
            wait(eng, sem, value)
            if not isinstance(value, int):
                eng.sem_inc(passed, 1)
        s_w_in = sem("s_w_in")
        s_w_hi = sem("s_w_hi")
        s_w_lo = sem("s_w_lo")
        s_in = sem("s_in")
        s_x1_in = sem("s_x1_in")
        s_gb_in = sem("s_gb_in")
        s_hi_done = sem("s_hi_done")
        s_lo_done = sem("s_lo_done")
        s_up_ready = sem("s_up_ready")
        s_gate_done = sem("s_gate_done")
        s_act_done = sem("s_act_done")
        a_hi_done = sem("a_hi_done")
        a_lo_done = sem("a_lo_done")
        s_down_ready = sem("s_down_ready")
        scaled_done = sem("scaled_done")
        base_done = sem("base_done")
        r_const = sem("r_const")
        r_step = sem("r_step")
        r_exp = sem("r_exp")
        mask_ready = sem("mask_ready")
        rank_ready = sem("rank_ready")
        slots_ready = sem("slots_ready")
        hot_lo_done = sem("hot_lo_done")
        hot_used = sem("hot_used")
        weights_in = [sem("weights_in0"), sem("weights_in1")]
        weights_ready = sem("weights_ready")
        gidx_done = sem("gidx_done")
        rows_in = [sem(f"rows_in{n}") for n in range(4)]
        xt_ready = sem("xt_ready")
        xt_copied = sem("xt_copied")
        gu_ready = sem("gu_ready")
        gate_done = sem("gate_done")
        inner_done = sem("inner_done")
        innerT_ready = sem("innerT_ready")
        innerT_copied = sem("innerT_copied")
        y_ready = sem("y_ready")
        y_copied = sem("y_copied")
        y_out = [sem(f"y_out{n}") for n in range(4)]
        ridx_done = sem("ridx_done")
        pair_in = [sem(f"pair_in{n}") for n in range(4)]
        gb2_in = sem("gb2_in")
        first_scaled = sem("first_scaled")
        pair_added = sem("pair_added")
        gated = sem("gated")
        result_done = sem("result_done")
        result_out = [sem(f"result_out{n}") for n in range(4)]

        stage = [probsT[:, :, :, :].rearrange("p a b c -> p a (b c)"), post[:, :, :]]
        CHUNKS = [("modT", 0), ("modT", 1), ("w", 0), ("w", 1), ("w", 2),
                  ("mod", 0), ("mod", 1), ("mod", 2), ("mod", 3), ("w", 3)]
        MOD_COLS = [2, 4, 3, 5]
        MOD_ROW = [GA, CB1, SB, GB]

        def batches(eng, body):
            body(Batch(0))
            with eng.Fori(1, NB - 1) as reg:
                body(Batch(None, reg))
            body(Batch(NB - 1))
            body(Batch(NB))

        def copy_transposed(eng, copy, b, c):
            wait(eng, pt_ready, b.lin(U, c + 1))
            wait(eng, av_done, b.lin(NG * TT, c // HG))
            copy(probsT[:, c % HG, :, :],
                 ps[:, PT_BANK + c % 2, :].rearrange("p (k n) -> p k n", k=TT)).then_inc(pt_free[c % 2], 1)

        ENGINES = 5

        def phase_over(eng, n):
            eng.drain().then_inc(phase_end, 1)
            eng.wait_ge(phase_end, ENGINES * n)

        def each_batch(eng, body):
            body(0)
            with eng.Fori(1, NB) as reg:
                body(reg)

        def count(b, per=1, off=0):
            return b * per + off

        def dyn(ap, first_dim, n):
            return ap[n] if isinstance(n, int) else ap[bass.ds(n, 1)].rearrange(first_dim)

        block = ctx.enter_context(nc.Block())

        @block.sync
        def _(sp):
            sp.dma_start(scT[:, :, :], cT_v).then_inc(const_in, 16)
            sp.dma_start(wr_raw[:, :, :], wr_v).then_inc(const_in, 16)
            sp.dma_start(rbias[:, :], r_bias.partition_broadcast(P)).then_inc(const_in, 16)
            sp.dma_start(V[0:NB, 3, :], b_out.partition_broadcast(NB)).then_inc(const_in, 16)

            def chunk(c):
                kind, i = CHUNKS[c]
                if c >= 2:
                    k0, i0 = CHUNKS[c - 2]
                    if k0 == "w":
                        sp.wait_ge(w_hi_done, i0 + 1)
                        sp.wait_ge(w_lo_done, i0 + 1)
                    else:
                        sp.wait_ge(dense_ready, place[(-1, k0, i0 if k0 == "mod" else 0)][1] + 1)
                src = (wmod_v[:, :, i * D:(i + 1) * D] if kind == "modT" else
                       wmod_v[:, :, MOD_COLS[i] * D:(MOD_COLS[i] + 1) * D] if kind == "mod" else
                       wqkv_v[:, :, i * D:(i + 1) * D] if i < 3 else wout_v)
                sp.dma_start(stage[c % 2], src).then_inc(chunk_in[c % 2], 16)

            chunk(0)
            chunk(1)
            sp.dma_start(xnat[:, :, :], x_t[0]).then_inc(x_in, 16)
            for c in range(2, 7):
                chunk(c)
            def stack(b, kind, i):
                which, dst, done = (0, qstack, q_stacked) if kind == "q" else (1, kstack, k_stacked)
                if b is None:
                    bank, _, uses = place[(-1, kind, i)]
                    wait(sp, dense_free[bank], uses + 1)
                else:
                    bank, _, uses = b.dense(kind, i)
                    g = i if i else NG
                    wait_apart(sp, dense_free[bank], uses + 1, passed_sp)
                    wait(sp, scores_ready, b.lin(U, UG * (g - 1)))
                for r in range(4):
                    half = half_lo if r in ((1, 3) if kind == "q" else (2, 3)) else half_hi
                    for j in range(HG):
                        sp.dma_start(dst[HD * r:HD * r + HD, i % 2, j, :].bitcast(f32),
                                     half[HD * j:HD * j + HD, which, :].bitcast(f32)).then_inc(done, 16)

            stack(None, "q", 0)
            stack(None, "k", 0)
            for c in range(7, len(CHUNKS)):
                chunk(c)
            for m, n in enumerate((2, 3, 4, 5)):
                sp.wait_ge(row_step, n)
                sp.dma_start(mod_d[MOD_ROW[m]], h2[0:NB, m, :]).then_inc(row_out, 16)
                if m == 0:
                    sp.dma_start(mod_d[GAB], V[0:NB, 2, :]).then_inc(row_out, 16)
            sp.wait_ge(row_out, 16 * NMOD)

            def body(b):
                if not b.after_last and not (b.reg is None and b.at == NB - 1):
                    if not b.first:
                        wait(sp, dense_ready, b.dense("v", 0)[1] - 2)
                    else:
                        wait(sp, dense_ready, place[(-1, "ht", KT - 1)][1] + 1)
                    sp.dma_start(xnat[:, :, :], x_t[b.lin(1, 1)] if b.reg is None else
                                 x_t[bass.ds(b.reg + 1, 1)].rearrange("a p t d -> p (a t) d")).then_inc(x_in, 16)
                if not b.first:
                    wait(sp, h2_step, b.lin(2 * TT, -2 * TT))
                    for n, m in enumerate((GA, GAB, CB1, SB)):
                        if b.reg is None:
                            row = mod_d[m, b.at - 1].partition_broadcast(P)
                        else:
                            row = mod_d[m, bass.ds(b.reg - 1, 1)].rearrange("a d -> (a d)").partition_broadcast(P)
                        sp.dma_start(bc[:, n, :], row).then_inc(bc_in, 16)

                def tile(t):
                    return b.lin(TT, t - TT)

                def load_x_again(t):
                    wait(sp, x1_done, b.lin(TT, max(t - 1, 0) - TT))
                    src = x_tile[tile(t)] if b.reg is None else \
                        x_tile[bass.ds(tile(t), 1)].rearrange("a p d -> p (a d)")
                    sp.dma_start(post[:, t % 2, :], src).then_inc(xr_in[t % 2], 16)

                if not b.first:
                    load_x_again(0)
                    load_x_again(1)
                for u in range(TAIL_END if b.after_last else U):
                    for kind, i in b.work(u, 1):
                        if kind in "qk":
                            stack(b, kind, i)
                        if kind == "tr":
                            bank, _, uses = b.dense(kind, i)
                            wait(sp, dense_free[bank], uses + 1)
                            dst = h2T_d[b.at - 1, i] if b.reg is None else \
                                h2T_d[bass.ds(b.reg - 1, 1), i].rearrange("a p n -> p (a n)")
                            sp.dma_start(dst, h2T[:, :, :].rearrange("p k n -> p (k n)")).then_inc(h2T_out, 16)
                    for kind, i in b.work(u, 2):
                        if kind == "out":
                            wait(sp, x1_done, b.lin(TT, i - TT + 1))
                            dst = x1_d[tile(i)] if b.reg is None else \
                                x1_d[bass.ds(tile(i), 1)].rearrange("a p d -> p (a d)")
                            sp.dma_start(dst, post[:, 2 + i % 2, :]).then_inc(x1_out[i % 2], 16)
                            if i + 2 < TT:
                                load_x_again(i + 2)
                    for kind, i in b.work(u, 6):
                        if kind == "out":
                            wait(sp, h2_step, b.lin(2 * TT, 2 * (i - TT + 1)))
                            dst = h2_d[P * tile(i):P * tile(i) + P] if b.reg is None else \
                                h2_d[bass.ds(P * tile(i), P)]
                            sp.dma_start(dst, h2[:, i, :]).then_inc(h2_out, 16)

            batches(sp, body)
            sp.wait_ge(h2T_out, 16 * NT)
            sp.wait_ge(h2_out, 16 * NT)
            for n in range(2):
                sp.wait_ge(x1_out[n], 16 * NT // 2)
            phase_over(sp, 1)

            sp.dma_start(sgu_raw[:, :, 0:FI], sWg.rearrange("(k p) i -> p k i", p=P)).then_inc(s_w_in, 16)
            sp.dma_start(sgu_raw[:, :, FI:], sWu.rearrange("(k p) i -> p k i", p=P)).then_inc(s_w_in, 16)
            sp.dma_start(swd_raw, sWd.rearrange("(m p) d -> p m d", p=P)).then_inc(s_w_in, 16)

            def load_expert(e):
                o = e % WSLOTS * WLEN
                gu = wslots[:, o:o + KT * 2 * FI].rearrange("p (k n) -> p k n", k=KT)
                dn = wslots[:, o + KT * 2 * FI:o + WLEN].rearrange("p (m d) -> p m d", m=MI)
                for dst, src in ((gu[:, :, 0:FI], Wg_v[e]), (gu[:, :, FI:], Wu_v[e]), (dn, Wd_v[e])):
                    sp.dma_start(dst, src).then_inc(weights_in[e % 2], 16)

            def shared_loads(b):
                wait(sp, s_hi_done, count(b))
                wait(sp, s_lo_done, count(b))
                src = h2T_d[b] if isinstance(b, int) else h2T_d[bass.ds(b, 1)].rearrange("a t p n -> (a t) p n")
                sp.dma_start(s_raw[:, :, :, :].rearrange("p t k n -> p t (k n)"),
                             src.rearrange("t p n -> p t n")).then_inc(s_in, 16)
                wait(sp, scaled_done, count(b, TT))
                row = mod_d[GB, b] if isinstance(b, int) else mod_d[GB, bass.ds(b, 1)].rearrange("a d -> (a d)")
                sp.dma_start(gbrow[:, :], row.partition_broadcast(P)).then_inc(s_gb_in, 16)
                if isinstance(b, int):
                    sp.wait_ge(s_w_lo, 2)
                sp.dma_start(base[:, bass.ds(b * TT, TT), :] if not isinstance(b, int) else
                             base[:, b * TT:(b + 1) * TT, :],
                             (x1_d[bass.ds(b * TT, TT)] if not isinstance(b, int) else
                              x1_d[b * TT:(b + 1) * TT]).rearrange("t p d -> p t d")).then_inc(s_x1_in, 16)
                if isinstance(b, int):
                    load_expert(0)
                    load_expert(1)

            each_batch(sp, shared_loads)
            phase_over(sp, 2)

            def loaded(e):
                sp.wait_ge(weights_in[e % 2], 48 * (e // 2 + 1))
                sp.sem_inc(weights_ready, 1)

            for e in range(2, NE):
                if e >= WSLOTS:
                    done = sp.value_load(freed_i[0:1, e - WSLOTS:e - WSLOTS + 1], min_val=1, max_val=NST + 1)
                    wait_apart(sp, y_ready, done, passed_sp)
                loaded(e - 2)
                load_expert(e)
            loaded(NE - 2)
            loaded(NE - 1)
            phase_over(sp, 3)

            def combine_loads(b):
                wait(sp, gated, count(b, TT))
                row = mod_d[GB, b] if isinstance(b, int) else mod_d[GB, bass.ds(b, 1)].rearrange("a d -> (a d)")
                sp.dma_start(gb2[:, :], row.partition_broadcast(P)).then_inc(gb2_in, 16)
                for t in range(TT):
                    wait(sp, result_done, count(b, TT, t + 1))
                    sp.dma_start(dyn(out_tile, "a p d -> p (a d)", b * TT + t), rows1[:, t, :])\
                        .then_inc(result_out[t], 16)

            each_batch(sp, combine_loads)
            for t in range(TT):
                sp.wait_ge(result_out[t], 16 * NB)

        @block.gpsimd
        def _(pool):
            nc.gpsimd.memset(minus_half[:, :], -0.5)
            nc.gpsimd.memset(ident[:, :], 0.0).then_inc(identity_ready, 1)
            pool.wait_ge(identity_ready, 1)
            nc.gpsimd.affine_select(out=ident[:, :], in_=ident[:, :], compare_op=ALU.not_equal, fill=1.0,
                                    base=0, pattern=[[-1, P]], channel_multiplier=1).then_inc(identity_ready, 1)

            def rstd_1(n):
                wait_apart(pool, ln1_step, n * 2 * TT, passed_pool)
                nc.gpsimd.tensor_scalar(rstd1[:, :], mv1[:, :, 1], EPS, None, ALU.add).then_inc(rstd1_step, 1)
                wait(pool, rstd1_step, n * 2 - 1)
                nc.gpsimd.tensor_tensor(rstd1[:, :], rstd1[:, :], minus_half[:, :], ALU.pow)\
                    .then_inc(rstd1_step, 1)

            def ht_low(n, k):
                wait(pool, ht_hi_done, n + 1)
                nc.gpsimd.tensor_tensor(hT_lo[:, k, :], ht_full[:, :], hT_hi[:, k, :],
                                        ALU.subtract).then_inc(ht_lo_done, 1)

            rstd_1(1)
            for k in range(KT):
                ht_low(k, k)

            def body(b):
                for u in range(TAIL_END if b.after_last else U):
                    if before(b, u, 2) and not scaled_by_vector(u - 2):
                        c = u - 2
                        wait(pool, factor_step, b.lin(3 * U, 3 * (c + 1)))
                        blocks = probs[:, c % 4, :].rearrange("p (k n) -> p k n", k=TT)
                        nc.gpsimd.tensor_tensor(blocks, blocks,
                                                factor[:, c % 4, :].unsqueeze(2).broadcast_to([P, TT, P]),
                                                ALU.mult).then_inc(scaled_p, 1)
                    for kind, i in b.work(u, 1):
                        if kind == "out":
                            wait(pool, xr_in[i % 2], b.lin(16 * TT // 2, 16 * (i // 2 + 1) - 16 * TT // 2))
                            if i == 0:
                                wait(pool, bc_in, b.lin(64, 0))
                            nc.gpsimd.tensor_tensor(post[:, i % 2, :], post[:, i % 2, :], bc[:, 1, :],
                                                    ALU.add).then_inc(xb_done, 1)
                            bank, _, uses = b.dense(kind, i)
                            wait(pool, dense_free[bank], uses + 1)
                            wait(pool, xb_done, b.lin(TT, i + 1 - TT))
                            nc.gpsimd.tensor_tensor(post[:, 2 + i % 2, :], post[:, 2 + i % 2, :],
                                                    post[:, i % 2, :], ALU.add).then_inc(x1_done, 1)
                        if kind == "tr":
                            bank, _, uses = b.dense(kind, i)
                            wait(pool, dense_free[bank], uses + 1)
                            nc.gpsimd.tensor_tensor(h2T_lo[:, :, :], h2T[:, :, :], h2T_hi[:, :, :],
                                                    ALU.subtract).then_inc(tr_lo_done, 1)
                        if kind == "ht":
                            ht_low(b.lin(KT, KT + i), i)
                    for kind, i in b.work(u, 3):
                        if kind == "out":
                            n2 = b.lin(2 * TT, 2 * (i - TT))
                            wait_apart(pool, ln2_step, n2 + 2, passed_pool)
                            rstd = rstd2[:, i % 2:i % 2 + 1]
                            nc.gpsimd.tensor_scalar(rstd, mv2[:, i % 2, 1:2], EPS, None, ALU.add)\
                                .then_inc(rstd2_step, 1)
                            wait(pool, rstd2_step, n2 + 1)
                            nc.gpsimd.tensor_tensor(rstd, rstd, minus_half[:, 0:1], ALU.pow)\
                                .then_inc(rstd2_step, 1)
                    for kind, i in b.work(u, 4):
                        if kind == "out":
                            n2 = b.lin(2 * TT, 2 * (i - TT))
                            wait(pool, h2_normal, b.lin(TT, i + 1 - TT))
                            nc.gpsimd.tensor_tensor(h2[:, i, :], h2[:, i, :], bc[:, 2, :],
                                                    ALU.mult).then_inc(h2_step, 1)
                            wait(pool, h2_step, n2 + 1)
                            nc.gpsimd.tensor_tensor(h2[:, i, :], h2[:, i, :], bc[:, 3, :],
                                                    ALU.add).then_inc(h2_step, 1)
                    if u == 36 and b.has("ht", 0) and not b.after_last:
                        rstd_1(b.lin(1, 2))

            batches(pool, body)
            phase_over(pool, 1)

            nc.gpsimd.memset(tri[:, :], 1.0).then_inc(r_const, 1)
            nc.gpsimd.memset(ones_b[:, :], 1.0).then_inc(r_const, 1)
            nc.gpsimd.memset(ones_te, 1.0).then_inc(r_const, 1)
            pool.wait_ge(r_const, 3)
            nc.gpsimd.affine_select(out=tri[:, :], in_=tri[:, :], compare_op=ALU.is_gt, fill=0.0, base=0,
                                    pattern=[[1, P]], channel_multiplier=-1).then_inc(r_const, 1)
            IMP = dict(allow_small_or_imprecise_dtypes=True)
            nc.gpsimd.iota(iota_e, [[1, NE]], base=0, channel_multiplier=0, **IMP).then_inc(r_const, 1)
            nc.gpsimd.iota(iota_t, [[1, NST]], base=0, channel_multiplier=0, **IMP).then_inc(r_const, 1)
            nc.gpsimd.iota(iota_p[:, :], [[1, P]], base=0, channel_multiplier=0, **IMP).then_inc(r_const, 1)
            nc.gpsimd.iota(tokid, [[P, NT]], base=0, channel_multiplier=1, **IMP).then_inc(r_const, 1)

            def shared_low(b):
                wait(pool, s_hi_done, count(b, 1, 1))
                nc.gpsimd.tensor_tensor(s_lo[:, :, :, :], s_raw[:, :, :, :], s_hi[:, :, :, :],
                                        ALU.subtract).then_inc(s_lo_done, 1)
                for m in range(MI):
                    wait(pool, a_hi_done, count(b, MI, m + 1))
                    nc.gpsimd.tensor_tensor(a_lo[:, m, :], s_act[:, m, :], a_hi[:, m, :],
                                            ALU.subtract).then_inc(a_lo_done, 1)
                for t in range(TT):
                    wait(pool, scaled_done, count(b, TT, t + 1))
                    if t == 0:
                        wait(pool, s_x1_in, count(b, 16, 16))
                    row = base[:, b * TT + t, :] if isinstance(b, int) else \
                        base[:, bass.ds(b * TT + t, 1), :].rearrange("p a d -> p (a d)")
                    nc.gpsimd.tensor_tensor(row, row, scaled[:, t % 2, :], ALU.add).then_inc(base_done, 1)

            each_batch(pool, shared_low)
            phase_over(pool, 2)

            def gather(i):
                for c in range(RING):
                    if not isinstance(i, int) or i > 0:
                        wait(pool, xt_ready, count(i, RING, c + 1 - RING))
                        wait(pool, rows_in[c], count(i, 16))
                    col = gather_i[:, c:c + 1] if isinstance(i, int) else gather_i[:, bass.ds(i * RING + c, 1)]
                    nc.gpsimd.tensor_copy(gidx[:, c:c + 1], col).then_inc(gidx_done, 1)
                    wait_apart(pool, gidx_done, count(i, RING, c + 1), passed_pool)
                    nc.gpsimd.indirect_dma_start(
                        out=xg[:, c, :], out_offset=None, in_=h2_d[:, :],
                        in_offset=bass.IndirectOffsetOnAxis(ap=gidx[:, c:c + 1], axis=0))\
                        .then_inc(rows_in[c], 16)

            gather(0)
            with pool.Fori(1, NST // RING) as reg:
                gather(reg)
            phase_over(pool, 3)

            def combine(b):
                for t in range(TT):
                    if not isinstance(b, int):
                        wait(pool, first_scaled, count(b, TT, t + 1 - TT))
                        wait(pool, result_out[t], count(b, 16))
                    col = slot_i[:, :, t:t + 1] if isinstance(b, int) else slot_i[:, :, bass.ds(b * TT + t, 1)]
                    nc.gpsimd.tensor_copy(ridx[:, :, t:t + 1], col).then_inc(ridx_done, 1)
                    wait_apart(pool, ridx_done, count(b, TT, t + 1), passed_pool)
                    for k, dst in enumerate((rows0, rows1)):
                        nc.gpsimd.indirect_dma_start(
                            out=dst[:, t, :], out_offset=None, in_=y_d[:, :],
                            in_offset=bass.IndirectOffsetOnAxis(ap=ridx[:, k, t:t + 1], axis=0))\
                            .then_inc(pair_in[t], 16)
                for t in range(TT):
                    wait(pool, pair_added, count(b, TT, t + 1))
                    if t == 0:
                        wait(pool, gb2_in, count(b, 16, 16))
                    nc.gpsimd.tensor_tensor(rows1[:, t, :], rows1[:, t, :], gb2[:, :], ALU.mult)\
                        .then_inc(gated, 1)

            each_batch(pool, combine)

        @block.scalar
        def _(act):
            act.wait_ge(const_in, 64)
            nc.scalar.activation(scT[:, :, :], scT[:, :, :], ACT.Silu).then_inc(silu_c_ready, 1)

            def weight_high(i):
                c = CHUNKS.index(("w", i))
                act.wait_ge(chunk_in[c % 2], 16 * (c // 2 + 1))
                dst = wqkv_hi[:, :, i * D:(i + 1) * D] if i < 3 else wout_hi[:, :, :]
                nc.scalar.copy(dst, stage[c % 2]).then_inc(w_hi_done, 1)

            def ht_high(bank, uses, k, hT_read):
                wait(act, dense_free[bank], uses + 1)
                if k == 0 and hT_read is not None:
                    wait(act, dense_ready, hT_read)
                nc.scalar.copy(hT_hi[:, k, :], ht_full[:, :]).then_inc(ht_hi_done, 1)

            def half_high(b, kind, i):
                which, done = (0, q_stacked) if kind == "q" else (1, k_stacked)
                if b is None:
                    bank, n, _ = place[(-1, kind, i)]
                    group = 0
                else:
                    bank, n, _ = b.dense(kind, i)
                    group = b.lin(NG, i if i else NG)
                wait(act, dense_ready, n + 1)
                wait(act, done, group * (256) if b is not None else 0)
                nc.scalar.activation(half_hi[:, which, :], ps[:, D_BANK + bank, :], ACT.Copy,
                                     scale=SCALE if kind == "q" else 1.0).then_inc(half_hi_done, 1)

            for i in range(3):
                weight_high(i)
            for k in range(KT):
                ht_high(*place[(-1, "ht", k)][::2], k, None)
            half_high(None, "q", 0)
            half_high(None, "k", 0)
            weight_high(3)
            nc.scalar.copy(wr_hi[:, :, :], wr_raw[:, :, :]).then_inc(w_hi_done, 1)

            def body(b):
                for u in range(TAIL_END if b.after_last else U):
                    if not b.after_last:
                        wait(act, max_ready, b.lin(U, u + 1))
                        wait(act, pt_ready, b.lin(U, u - 3))
                        for k in range(TT):
                            last = nc.scalar.activation(
                                probs[:, u % 4, k * P:(k + 1) * P], ps[:, S_BANK + u % 2, k * P:(k + 1) * P],
                                ACT.Exp, bias=neg_max[:, u % 4, k:k + 1], scale=1.0,
                                accum_out=sums[:, u % 4, k:k + 1])
                        last.then_inc(exp_done, 1)
                        nc.scalar.activation(weight[:, u % 4, :], neg_max[:, u % 4, :], ACT.Exp,
                                             bias=neg_top[:, u % 4:u % 4 + 1], scale=-1.0)\
                            .then_inc(weight_done, 1)
                    if before(b, u, LAG) and (u - LAG) % 4 == 3:
                        copy_transposed(act, nc.scalar.copy, b, u - LAG)
                    if u % UG == 4 and before(b, u, UG):
                        g = (u // UG - 1) % NG
                        wait(act, av_done, b.lin(NG * TT, TT * (u // UG)))
                        if g == 0:
                            if not b.first:
                                wait(act, dense_ready, b.dense("out", TT - 1)[1] + 1)
                        nc.scalar.copy(outT_hi[:, g, :], ps[:, AV_BANK, :]).then_inc(out_hi_done, 1)
                    for kind, i in b.work(u, 1):
                        bank, n, uses = b.dense(kind, i)
                        if kind == "v":
                            wait(act, dense_ready, n + 1)
                            wait(act, av_done, b.lin(NG * TT, 0))
                            if b.first and i == 0:
                                act.wait_ge(row_out, 16 * NMOD)
                            nc.scalar.copy(V[:, i, :], ps[:, D_BANK + bank, :]).then_inc(dense_free[bank], 1)
                        if kind in "qk":
                            half_high(b, kind, i)
                        if kind == "tr":
                            wait(act, dense_ready, n + 1)
                            wait(act, h2T_out, b.lin(16 * TT, 16 * (i - TT)))
                            wait(act, tr_lo_done, b.lin(TT, i - TT))
                            nc.scalar.copy(h2T[:, :, :], ps[:, D_BANK + bank, :].rearrange("p (k n) -> p k n", k=KT))
                            if i:
                                wait(act, dense_ready, b.dense("route", i - 1)[1] + 1)
                            else:
                                wait(act, dense_ready, b.dense("out", 0)[1])
                            nc.scalar.copy(h2T_hi[:, :, :], ps[:, D_BANK + bank, :].rearrange("p (k n) -> p k n", k=KT))\
                                .then_inc(dense_free[bank], 1)
                        if kind == "ht":
                            ht_high(bank, uses, i, b.dense("k", NG - 1)[1] + 1)

            batches(act, body)
            phase_over(act, 1)

            act.wait_ge(s_w_in, 48)
            nc.scalar.copy(sgu_hi[:, :, :], sgu_raw).then_inc(s_w_hi, 1)
            nc.scalar.copy(swd_hi[:, :, :], swd_raw).then_inc(s_w_hi, 1)

            def shared_act(b):
                wait(act, s_in, count(b, 16, 16))
                wait(act, s_up_ready, count(b, 2 * MI))
                nc.scalar.copy(s_hi[:, :, :, :], s_raw[:, :, :, :]).then_inc(s_hi_done, 1)
                for m in range(MI):
                    wait(act, s_up_ready, count(b, 2 * MI, 2 * m + 1))
                    nc.scalar.activation(s_gate[:, m, :], ps[:, 2 * m, :], ACT.Silu).then_inc(s_gate_done, 1)
                for m in range(MI):
                    wait(act, s_act_done, count(b, MI, m + 1))
                    wait(act, s_down_ready, count(b, TT))
                    nc.scalar.copy(a_hi[:, m, :], s_act[:, m, :]).then_inc(a_hi_done, 1)

            shared_act(0)
            act.wait_ge(r_step, 2)
            nc.scalar.activation(prob, prob, ACT.Exp).then_inc(r_exp, 1)
            with act.Fori(1, NB) as reg:
                shared_act(reg)
            phase_over(act, 2)

            def store(c, i):
                wait(act, y_copied, count(i, RING, c + 1))
                dst = y_d[c * P:(c + 1) * P] if isinstance(i, int) and i == 0 else \
                    y_d[bass.ds(i * (RING * P) + c * P, P)] if not isinstance(i, int) else \
                    y_d[(i * RING + c) * P:(i * RING + c + 1) * P]
                act.dma_start(dst, yrow[:, c, :]).then_inc(y_out[c], 16)

            def routed_act(i):
                for c in range(RING):
                    wait(act, xt_ready, count(i, RING, c + 1))
                    wait(act, gu_ready, count(i, RING, c - 1))
                    nc.scalar.copy(xT[:, c % 2, :, :],
                                   ps[:, c % 2, :].rearrange("p (k n) -> p k n", k=KT)).then_inc(xt_copied, 1)
                    wait(act, gu_ready, count(i, RING, c + 1))
                    wait(act, inner_done, count(i, RING, c - 1))
                    nc.scalar.activation(gate[:, c % 2, :], ps[:, 2 + c % 2, 0:FI], ACT.Silu)\
                        .then_inc(gate_done, 1)
                    if c >= 2:
                        store(c - 2, i)
                    elif not isinstance(i, int):
                        store(c + 2, i - 1)

            routed_act(0)
            with act.Fori(1, NST // RING) as reg:
                routed_act(reg)
            store(2, NST // RING - 1)
            store(3, NST // RING - 1)
            for c in range(RING):
                act.wait_ge(y_out[c], 16 * NST // RING)
            phase_over(act, 3)

            def combine_act(b):
                for t in range(TT):
                    wait(act, pair_in[t], count(b, 32, 32))
                    w = wts[:, 0, t:t + 1] if isinstance(b, int) else wts[:, 0, bass.ds(b * TT + t, 1)]
                    nc.scalar.activation(rows0[:, t, :], rows0[:, t, :], ACT.Copy, scale=w)\
                        .then_inc(first_scaled, 1)

            each_batch(act, combine_act)

        @block.vector
        def _(dve):
            def weight_low(i):
                c = CHUNKS.index(("w", i))
                dve.wait_ge(w_hi_done, i + 1)
                hi, lo = ((w[:, :, i * D:(i + 1) * D] for w in (wqkv_hi, wqkv_lo)) if i < 3
                          else (wout_hi[:, :, :], wout_lo[:, :, :]))
                nc.vector.tensor_tensor(lo, stage[c % 2], hi, ALU.subtract).then_inc(w_lo_done, 1)

            def ln1_stats(need_x, t):
                wait(dve, x_in, need_x)
                nc.vector.bn_stats(stats1[:, t, :], xnat[:, t, :]).then_inc(ln1_step, 1)

            def ln1_mean(n9):
                wait_apart(dve, ln1_step, n9 + TT, passed_dve)
                for t in range(TT):
                    nc.vector.bn_aggr(mv1[:, t, :], stats1[:, t, :]).then_inc(ln1_step, 1)

            def normalize1(n, t):
                wait(dve, rstd1_step, n * 2)
                nc.vector.tensor_scalar(xnat[:, t, :], xnat[:, t, :], mv1[:, t, 0:1], rstd1[:, t:t + 1],
                                        ALU.subtract, ALU.mult).then_inc(xn_done, 1)

            def ht_whole(n, k, place_of, nb):
                bank, at, _ = place_of
                wait(dve, dense_ready, at + 1)
                wait(dve, ht_lo_done, n)
                if isinstance(nb, int):
                    ca, sa = modT[:, 1, k, nb:nb + 1], modT[:, 0, k, nb:nb + 1]
                else:
                    ca, sa = modT[:, 1, k, bass.ds(nb, 1)], modT[:, 0, k, bass.ds(nb, 1)]
                nc.vector.tensor_scalar(ht_full[:, :], ps[:, D_BANK + bank, :], ca, sa, ALU.mult,
                                        ALU.add).then_inc(dense_free[bank], 1)

            def half_low(b, kind, i):
                which = 0 if kind == "q" else 1
                bank = (place[(-1, kind, i)] if b is None else b.dense(kind, i))[0]
                before = 0 if b is None else b.lin(2 * NG, 2 * (i if i else NG))
                wait(dve, half_hi_done, before + which + 1)
                nc.vector.scalar_tensor_tensor(half_lo[:, which, :], ps[:, D_BANK + bank, :],
                                               SCALE if kind == "q" else 1.0, half_hi[:, which, :],
                                               ALU.mult, ALU.subtract).then_inc(dense_free[bank], 1)

            bank, at, _ = place[(-1, "modT", 0)]
            dve.wait_ge(dense_ready, at + 1)
            cols = ps[:, D_BANK + bank, 0:2 * KT * NB].rearrange("p (m k b) -> p m k b", m=2, k=KT)
            nc.vector.tensor_copy(modT[:, 0, :, :], cols[:, 0, :, :])
            nc.vector.tensor_scalar_add(modT[:, 1, :, :], cols[:, 1, :, :], 1.0).then_inc(dense_free[bank], 1)
            dve.wait_ge(dense_free[bank], 1)
            for t in range(TT):
                ln1_stats(16, t)
            ln1_mean(0)
            for t in range(TT):
                normalize1(1, t)
            for i in range(2):
                weight_low(i)
            for k in range(KT):
                ht_whole(k, k, place[(-1, "ht", k)], 0)
            weight_low(2)
            half_low(None, "q", 0)
            half_low(None, "k", 0)
            dve.wait_ge(const_in, 64)
            for m in range(4):
                bank, at, uses = place[(-1, "mod", m)]
                dve.wait_ge(dense_ready, at + 1)
                got = ps[0:NB, D_BANK + bank, :]
                if m in (0, 3):
                    nc.vector.tensor_scalar(V[0:NB, 0, :], got, 0.0, 2.0, ALU.is_ge, ALU.mult)
                    nc.vector.tensor_scalar(V[0:NB, 1, :], got, -1.0, None, ALU.mult).then_inc(gate_step, 1)
                    dve.wait_ge(gate_step, 3 * (m // 3) + 1)
                    nc.vector.tensor_tensor(V[0:NB, 1, :], got, V[0:NB, 1, :], ALU.max)\
                        .then_inc(dense_free[bank], 1)
                    dve.wait_ge(dense_free[bank], uses + 1)
                    nc.vector.tensor_scalar_max(V[0:NB, 1, :], V[0:NB, 1, :], 0.25).then_inc(gate_step, 1)
                    dve.wait_ge(gate_step, 3 * (m // 3) + 2)
                    nc.vector.tensor_scalar_add(V[0:NB, 0, :], V[0:NB, 0, :], -1.0).then_inc(gate_step, 1)
                    dve.wait_ge(gate_step, 3 * (m // 3) + 3)
                    nc.vector.tensor_tensor(h2[0:NB, m, :], V[0:NB, 0, :], V[0:NB, 1, :],
                                            ALU.mult).then_inc(row_step, 1)
                    if m == 0:
                        dve.wait_ge(row_step, 1)
                        nc.vector.tensor_tensor(V[0:NB, 2, :], h2[0:NB, 0, :], V[0:NB, 3, :],
                                                ALU.mult).then_inc(row_step, 1)
                else:
                    nc.vector.tensor_scalar_add(h2[0:NB, m, :], got, 1.0 if m == 1 else 0.0)\
                        .then_inc(row_step, 1)
                    dve.wait_ge(row_step, m + 2)
                    dve.sem_inc(dense_free[bank], 1)
            weight_low(3)
            dve.wait_ge(w_hi_done, 5)
            nc.vector.tensor_tensor(wr_lo[:, :, :], wr_raw[:, :, :], wr_hi[:, :, :],
                                    ALU.subtract).then_inc(w_lo_done, 1)

            def body(b):
                for u in range(TAIL_END if b.after_last else U):
                    if not b.after_last:
                        wait(dve, scores_ready, b.lin(U, u + 1))
                        wait(dve, weight_done, b.lin(U, u - 3))
                        nc.vector.reduce_max(neg_max[:, u % 4, :],
                                             ps[:, S_BANK + u % 2, :].rearrange("p (k n) -> p k n", k=TT), AX.X,
                                             negate=True).then_inc(block_max_done, 1)
                        wait(dve, block_max_done, b.lin(U, u + 1))
                        nc.vector.tensor_reduce(neg_top[:, u % 4:u % 4 + 1], neg_max[:, u % 4, :], AX.X,
                                                ALU.min).then_inc(max_ready, 1)
                    if before(b, u, 2):
                        c = u - 2
                        n = b.lin(3 * U, 3 * c)
                        wait(dve, weight_done, b.lin(U, c + 1))
                        nc.vector.scalar_tensor_tensor(weighed[:, c % 4, :], weight[:, c % 4, :], 1.0,
                                                       sums[:, c % 4, :], ALU.mult, ALU.mult,
                                                       accum_out=total[:, c % 4:c % 4 + 1])\
                            .then_inc(factor_step, 1)
                        wait(dve, factor_step, n + 1)
                        nc.vector.reciprocal(total[:, c % 4:c % 4 + 1], total[:, c % 4:c % 4 + 1])\
                            .then_inc(factor_step, 1)
                        wait(dve, factor_step, n + 2)
                        nc.vector.tensor_scalar(factor[:, c % 4, :], weighed[:, c % 4, :],
                                                total[:, c % 4:c % 4 + 1], None, ALU.mult)\
                            .then_inc(factor_step, 1)
                        if scaled_by_vector(c):
                            wait(dve, factor_step, n + 3)
                            for k in range(TT):
                                part = probs[:, c % 4, k * P:(k + 1) * P]
                                last = nc.vector.tensor_scalar(part, part, factor[:, c % 4, k:k + 1], None,
                                                               ALU.mult)
                            last.then_inc(scaled_v, 1)
                    if before(b, u, LAG) and (u - LAG) % 4 != 3:
                        copy_transposed(dve, nc.vector.tensor_copy, b, u - LAG)
                    if u % UG == 4 and before(b, u, UG):
                        g = (u // UG - 1) % NG
                        wait(dve, out_hi_done, b.lin(NG, u // UG))
                        nc.vector.tensor_tensor(outT_lo[:, g, :], ps[:, AV_BANK, :], outT_hi[:, g, :],
                                                ALU.subtract).then_inc(av_free, 1)
                    for kind, i in b.work(u, 1):
                        bank, n, uses = b.dense(kind, i)
                        if kind in "qk":
                            half_low(b, kind, i)
                        if kind == "out":
                            wait(dve, dense_ready, n + 1)
                            if i == 0:
                                wait(dve, bc_in, b.lin(64, 0))
                            wait(dve, x1_out[i % 2], b.lin(16 * TT // 2, 16 * (i // 2) - 16 * TT // 2))
                            wait(dve, h2_normal, b.lin(TT, max(i - 1, 0) - TT))
                            nc.vector.tensor_tensor(post[:, 2 + i % 2, :], ps[:, D_BANK + bank, :], bc[:, 0, :],
                                                    ALU.mult).then_inc(dense_free[bank], 1)
                        if kind == "route":
                            wait(dve, dense_ready, n + 1)
                            dst = logits[:, TT * (b.at - 1) + i, :] if b.reg is None else \
                                logits[:, bass.ds(b.lin(TT, i - TT), 1), :].rearrange("p a e -> p (a e)")
                            nc.vector.tensor_tensor(dst, ps[:, D_BANK + bank, 0:NE], rbias[:, :],
                                                    ALU.add).then_inc(dense_free[bank], 1)
                        if kind == "ht":
                            ht_whole(b.lin(KT, KT + i), i, b.dense(kind, i), b.lin(1, 1))
                    for kind, i in b.work(u, 3):
                        if kind == "out":
                            n2 = b.lin(2 * TT, 2 * (i - TT))
                            wait(dve, x1_done, b.lin(TT, i - TT + 1))
                            nc.vector.bn_stats(stats2[:, i % 2, :], post[:, 2 + i % 2, :]).then_inc(ln2_step, 1)
                            wait_apart(dve, ln2_step, n2 + 1, passed_dve)
                            nc.vector.bn_aggr(mv2[:, i % 2, :], stats2[:, i % 2, :]).then_inc(ln2_step, 1)
                    for kind, i in b.work(u, 4):
                        if kind == "out":
                            wait(dve, rstd2_step, b.lin(2 * TT, 2 * (i + 1 - TT)))
                            if i == 0:
                                wait(dve, h2_out, b.lin(16 * TT, -16 * TT))
                                wait(dve, tr_lo_done, b.lin(TT, -TT))
                            nc.vector.tensor_scalar(h2[:, i, :], post[:, 2 + i % 2, :], mv2[:, i % 2, 0:1],
                                                    rstd2[:, i % 2:i % 2 + 1], ALU.subtract,
                                                    ALU.mult).then_inc(h2_normal, 1)
                    if not b.after_last and b.has("ht", 0):
                        n9 = b.lin(2 * TT, 2 * TT)
                        if 30 <= u < 30 + TT:
                            ln1_stats(b.lin(16, 32), u - 30)
                        if u == 35:
                            ln1_mean(n9)
                        if 38 <= u < 38 + TT:
                            normalize1(b.lin(1, 2), u - 38)

            batches(dve, body)
            phase_over(dve, 1)

            for n, (lo, raw, hi) in enumerate(((sgu_lo, sgu_raw, sgu_hi), (swd_lo, swd_raw, swd_hi))):
                dve.wait_ge(s_w_hi, n + 1)
                nc.vector.tensor_tensor(lo[:, :, :], raw, hi[:, :, :], ALU.subtract).then_inc(s_w_lo, 1)

            def shared_dve(b):
                for m in range(MI):
                    wait(dve, s_gate_done, count(b, MI, m + 1))
                    wait(dve, s_up_ready, count(b, 2 * MI, 2 * m + 2))
                    wait(dve, a_lo_done, count(b, MI))
                    nc.vector.tensor_tensor(s_act[:, m, :], s_gate[:, m, :], ps[:, 2 * m + 1, :],
                                            ALU.mult).then_inc(s_act_done, 1)
                wait(dve, s_gb_in, count(b, 16, 16))
                for t in range(TT):
                    wait(dve, s_down_ready, count(b, TT, t + 1))
                    wait(dve, base_done, count(b, TT, t - 1))
                    nc.vector.tensor_tensor(scaled[:, t % 2, :], ps[:, 4 + t, :], gbrow[:, :],
                                            ALU.mult).then_inc(scaled_done, 1)

            shared_dve(0)

            step = [0]

            def then(ins):
                step[0] += 1
                ins.then_inc(r_step, 1)
                dve.wait_ge(r_step, step[0])

            def te(v):
                return v.rearrange("p (t e) -> p t e", e=NE)

            def over_e(v):
                return v.unsqueeze(2).broadcast_to([P, NT, NE])

            L = logits[:, :, :]
            experts = iota_e.unsqueeze(1).broadcast_to([P, NT, NE])
            then(nc.vector.reduce_max(row_max, L, AX.X))
            then(nc.vector.tensor_tensor(te(prob), L, over_e(row_max), ALU.subtract))
            dve.wait_ge(r_exp, 1)
            then(nc.vector.reduce_sum(row_sum, te(prob), AX.X))
            then(nc.vector.reciprocal(row_sum, row_sum))
            then(nc.vector.tensor_tensor(te(prob), te(prob), over_e(row_sum), ALU.mult))
            dve.wait_ge(r_const, 8)
            left = prob
            for k in range(2):
                then(nc.vector.reduce_max(top[k], te(left), AX.X))
                then(nc.vector.tensor_tensor(te(eq), te(left), over_e(top[k]), ALU.is_equal))
                then(nc.vector.scalar_tensor_tensor(te(order), te(eq), -float(NE), experts, ALU.mult, ALU.add))
                then(nc.vector.tensor_reduce(first, te(order), AX.X, ALU.min))
                then(nc.vector.tensor_tensor(te(oh[k]), te(order), over_e(first), ALU.is_equal))
                if k == 0:
                    then(nc.vector.scalar_tensor_tensor(slot_of, oh[0], -2.0, prob, ALU.mult, ALU.add))
                    left = slot_of
            nc.vector.tensor_tensor(mask[:, :], oh[0], oh[1], ALU.add).then_inc(mask_ready, 1)
            then(nc.vector.tensor_tensor(den, top[0], top[1], ALU.add))
            then(nc.vector.tensor_scalar_add(den, den, 1e-9))
            then(nc.vector.reciprocal(den, den))
            for k in range(2):
                then(nc.vector.tensor_tensor(wts[:, k, :], top[k], den, ALU.mult))
            dve.wait_ge(rank_ready, 1)
            then(nc.vector.tensor_copy(tot_e.rearrange("p (e t) -> p e t", e=NE),
                                       ps[:, 1, :].rearrange("p (t e) -> p e t", e=NE)))
            then(nc.vector.tensor_tensor_scan(run, ones_te, tot_e, 0.0, ALU.mult, ALU.add))
            ends = run.rearrange("p (e t) -> p e t", e=NE)[:, :, NT - 1]
            then(nc.vector.memset(cum_prev, 0.0))
            then(nc.vector.tensor_copy(cum_prev[:, 1:NE], ends[:, 0:NE - 1]))
            then(nc.vector.tensor_tensor(cnt, ends, cum_prev, ALU.subtract))
            then(nc.vector.tensor_scalar_add(tiles_i, cnt, float(P - 1)))
            then(nc.vector.tensor_scalar(tiles_i, tiles_i, 7, None, ALU.logical_shift_right))
            then(nc.vector.tensor_copy(tiles, tiles_i))
            then(nc.vector.tensor_tensor_scan(tiles_cum, ones_te[:, 0:NE], tiles, 0.0, ALU.mult, ALU.add))
            then(nc.vector.tensor_tensor(offset, tiles_cum, tiles, ALU.subtract))
            then(nc.vector.scalar_tensor_tensor(offset, offset, float(P), cum_prev, ALU.mult, ALU.subtract))
            then(nc.vector.tensor_tensor(run, run, tot_e, ALU.subtract))
            then(nc.vector.tensor_tensor(run.rearrange("p (e t) -> p e t", e=NE),
                                         run.rearrange("p (e t) -> p e t", e=NE),
                                         offset.unsqueeze(2).broadcast_to([P, NE, NT]), ALU.add))
            then(nc.vector.tensor_tensor(te(slot_of), te(ps[:, 0, :]),
                                         run.rearrange("p (e t) -> p t e", e=NE), ALU.add))
            dve.sem_inc(slots_ready, 1)
            for k in range(2):
                then(nc.vector.tensor_tensor(eq, slot_of, oh[k], ALU.mult))
                then(nc.vector.reduce_sum(slots[:, k * NT:(k + 1) * NT], te(eq), AX.X))
            then(nc.vector.tensor_copy(slot_i[:, :, :].rearrange("p k t -> p (k t)"), slots))
            si = slot_i[:, :, :].rearrange("p k t -> p (k t)")
            then(nc.vector.tensor_scalar(tmp_i, si, 7, None, ALU.logical_shift_right))
            then(nc.vector.tensor_scalar(tmp2_i, si, P - 1, None, ALU.bitwise_and))
            then(nc.vector.tensor_copy(slots_hi, tmp_i))
            then(nc.vector.tensor_copy(slots_lo, tmp2_i))
            big = wslots[:, 2 * WLEN:2 * WLEN + NST * NE].rearrange("p (t e) -> p t e", e=NE)
            then(nc.vector.tensor_tensor(big, iota_t.unsqueeze(2).broadcast_to([P, NST, NE]),
                                         tiles_cum.unsqueeze(1).broadcast_to([P, NST, NE]), ALU.is_ge))
            then(nc.vector.reduce_sum(e_tab, big, AX.X))
            then(nc.vector.tensor_scalar_min(e_tab, e_tab, float(NE - 1)))
            then(nc.vector.tensor_copy(e_tab_i, e_tab))
            then(nc.vector.tensor_scalar_add(need_i[0:1, :], e_tab[0:1, :], 1.0))
            then(nc.vector.tensor_scalar(e_tab_i, e_tab_i, WSLOTS - 1, None, ALU.bitwise_and))
            then(nc.vector.tensor_copy(e_tab, e_tab_i))
            then(nc.vector.tensor_scalar(woff_i[0:1, :], e_tab[0:1, :], float(WLEN), None, ALU.mult))
            then(nc.vector.tensor_scalar_add(freed_i[0:1, :], tiles_cum[0:1, :], 1.0))

            with dve.Fori(1, NB) as reg:
                shared_dve(reg)

            for n in range(2 * NT):
                if n >= 2:
                    dve.wait_ge(hot_used, n - 1)
                nc.vector.tensor_scalar(hot_lo[:, n % 2, :], iota_p[:, :], slots_lo[:, n:n + 1], None,
                                        ALU.is_equal).then_inc(hot_lo_done, 1)
                nc.vector.tensor_scalar(hot_hi[:, n % 2, :], iota_t, slots_hi[:, n:n + 1],
                                        tokid[:, n % NT:n % NT + 1], ALU.is_equal, ALU.mult)\
                    .then_inc(hot_lo_done, 1)
            dve.wait_ge(hot_used, 2 * NT)
            nc.vector.tensor_copy(gather_i[:, :], ps[:, 0, 0:NST])
            phase_over(dve, 2)

            def routed_dve(i):
                for c in range(RING):
                    wait(dve, gate_done, count(i, RING, c + 1))
                    wait(dve, innerT_ready, count(i, RING, c - 1))
                    nc.vector.tensor_tensor(inner[:, c % 2, :], gate[:, c % 2, :], ps[:, 2 + c % 2, FI:],
                                            ALU.mult).then_inc(inner_done, 1)
                    if c or not isinstance(i, int):
                        y_copy(c - 1 if c else RING - 1, i if c else i - 1)
                    wait(dve, innerT_ready, count(i, RING, c + 1))
                    wait(dve, y_ready, count(i, RING, c))
                    nc.vector.tensor_copy(innerT[:, c % 2, :, :],
                                          ps[:, 4 + c % 2, 0:MI * P].rearrange("p (m n) -> p m n", m=MI))\
                        .then_inc(innerT_copied, 1)

            def y_copy(c, i):
                wait(dve, y_ready, count(i, RING, c + 2))
                wait(dve, y_out[c], count(i, 16))
                nc.vector.tensor_copy(yrow[:, c, :], ps[:, 6 + c % 2, :]).then_inc(y_copied, 1)

            routed_dve(0)
            with dve.Fori(1, NST // RING) as reg:
                routed_dve(reg)
            y_copy(RING - 1, NST // RING - 1)
            phase_over(dve, 3)

            def combine_dve(b):
                for t in range(TT):
                    wait(dve, first_scaled, count(b, TT, t + 1))
                    w = wts[:, 1, t:t + 1] if isinstance(b, int) else wts[:, 1, bass.ds(b * TT + t, 1)]
                    nc.vector.scalar_tensor_tensor(rows1[:, t, :], rows1[:, t, :], w, rows0[:, t, :],
                                                   ALU.mult, ALU.add).then_inc(pair_added, 1)
                for t in range(TT):
                    wait(dve, gated, count(b, TT, t + 1))
                    row = base[:, b * TT + t, :] if isinstance(b, int) else \
                        base[:, bass.ds(b * TT + t, 1), :].rearrange("p a d -> p (a d)")
                    nc.vector.tensor_tensor(rows1[:, t, :], rows1[:, t, :], row, ALU.add)\
                        .then_inc(result_done, 1)

            each_batch(dve, combine_dve)

        @block.tensor
        def _(pe):
            def three(out_ap, lhs_hi, lhs_lo, rhs_hi, rhs_lo, start, stop):
                nc.tensor.matmul(out_ap, lhs_hi, rhs_hi, start=start, stop=False)
                nc.tensor.matmul(out_ap, lhs_lo, rhs_hi, start=False, stop=False)
                return nc.tensor.matmul(out_ap, lhs_hi, rhs_lo, start=False, stop=stop)

            def dense(b, kind, i):
                bank, n, uses = place[(-1, kind, i)] if b is None else b.dense(kind, i)
                wait(pe, dense_free[bank], uses)
                to = ps[:, D_BANK + bank, :]
                if kind == "modT":
                    pe.wait_ge(silu_c_ready, 1)
                    for m in range(2):
                        pe.wait_ge(chunk_in[m], 16)
                        for kt in range(KT):
                            for k in range(KT):
                                last = nc.tensor.matmul(to[:, (m * KT + kt) * NB:(m * KT + kt + 1) * NB],
                                                        stage[m][:, k, kt * P:(kt + 1) * P], scT[:, k, :],
                                                        start=k == 0, stop=k == KT - 1)
                elif kind == "mod":
                    c = CHUNKS.index((kind, i))
                    pe.wait_ge(chunk_in[c % 2], 16 * (c // 2 + 1))
                    for k in range(KT):
                        last = nc.tensor.matmul(to[0:NB, :], scT[:, k, :], stage[c % 2][:, k, :],
                                                start=k == 0, stop=k == KT - 1)
                elif kind == "ht":
                    if i == 0:
                        pe.wait_ge(identity_ready, 2)
                        wait(pe, xn_done, TT if b is None else b.lin(TT, 2 * TT))
                    for t in range(TT):
                        last = nc.tensor.transpose(to[:, t * P:(t + 1) * P], xnat[:, t, i * P:(i + 1) * P],
                                                   ident[:, :])
                elif kind in "qk":
                    col = i * P + (0 if kind == "q" else D)
                    if kind == "q" and i == 0:
                        wait(pe, ht_lo_done, KT if b is None else b.lin(KT, 2 * KT))
                    if b is None:
                        pe.wait_ge(w_lo_done, 1 if kind == "q" else 2)
                    for k in range(KT):
                        last = three(to, wqkv_hi[:, k, col:col + P], wqkv_lo[:, k, col:col + P],
                                     hT_hi[:, k, :], hT_lo[:, k, :], k == 0, k == KT - 1)
                elif kind == "v":
                    if b.first and i == 0:
                        pe.wait_ge(w_lo_done, 3)
                    for k in range(KT):
                        at = slice(i * P, (i + 1) * P)
                        last = three(to, hT_hi[:, k, at], hT_lo[:, k, at],
                                     wqkv_hi[:, k, 2 * D:], wqkv_lo[:, k, 2 * D:], k == 0, k == KT - 1)
                elif kind == "out":
                    if i == 0:
                        wait(pe, av_free, b.lin(NG, 0))
                        pe.wait_ge(w_lo_done, 5)
                    at = slice(i * P, (i + 1) * P)
                    for k in range(KT):
                        last = three(to, outT_hi[:, k, at], outT_lo[:, k, at],
                                     wout_hi[:, k, :], wout_lo[:, k, :], k == 0, k == KT - 1)
                elif kind == "tr":
                    wait(pe, h2_step, b.lin(2 * TT, 2 * (i + 1 - TT)))
                    for k in range(KT):
                        last = nc.tensor.transpose(to[:, k * P:(k + 1) * P], h2[:, i, k * P:(k + 1) * P],
                                                   ident[:, :])
                elif kind == "route":
                    wait(pe, tr_lo_done, b.lin(TT, i + 1 - TT))
                    for k in range(KT):
                        last = three(to[:, 0:NE], h2T_hi[:, k, :], h2T_lo[:, k, :],
                                     wr_hi[:, k, :], wr_lo[:, k, :], k == 0, k == KT - 1)
                last.then_inc(dense_ready, 1)

            for kind, i in PRO:
                dense(None, kind, i)

            def body(b):
                for u in range(TAIL_END if b.after_last else U):
                    g, t, j = u // UG, u // HG % TT, u % HG
                    if not b.after_last:
                        if u % UG == 0:
                            wait(pe, q_stacked, b.lin(256 * NG, 256 * (g + 1)))
                            wait(pe, k_stacked, b.lin(256 * NG, 256 * (g + 1)))
                        wait(pe, exp_done, b.lin(U, u - 1))
                        nc.tensor.matmul(ps[:, S_BANK + u % 2, :], qstack[:, g % 2, j, t * P:(t + 1) * P],
                                         kstack[:, g % 2, j, :], start=True, stop=True)\
                            .then_inc(scores_ready, 1)
                    if before(b, u, LAG):
                        c = u - LAG
                        wait_scaled(pe, b, c, scaled_v, scaled_p)
                        wait(pe, pt_free[c % 2], b.lin(U // 2, c // 2))
                        for k in range(TT):
                            last = nc.tensor.transpose(ps[:, PT_BANK + c % 2, k * P:(k + 1) * P],
                                                       probs[:, c % 4, k * P:(k + 1) * P], ident[:, :])
                        last.then_inc(pt_ready, 1)
                    if (u - AV_AT) % HG == 0 and before(b, u, AV_AT):
                        n = (u - AV_AT) // HG
                        if n == 0:
                            for i in (TT - 1, 1, 2):
                                bank, _, uses = b.dense("v", i)
                                wait(pe, dense_free[bank], uses + 1)
                        if n % TT == 0:
                            wait(pe, av_free, b.lin(NG, n // TT))
                        for slot in range(2):
                            wait(pe, pt_free[slot], b.lin(U // 2, (n + 1) * HG // 2))
                        vg = n // TT % NG
                        for k in range(TT):
                            for j in range(HG):
                                last = nc.tensor.matmul(
                                    ps[HD * j:HD * j + HD, AV_BANK, n % TT * P:n % TT * P + P],
                                    V[:, k, vg * P + HD * j:vg * P + HD * j + HD], probsT[:, j, k, :],
                                    start=k == 0, stop=k == TT - 1)
                        last.then_inc(av_done, 1)
                    for kind, i in b.work(u):
                        dense(b, kind, i)

            batches(pe, body)
            phase_over(pe, 1)

            def shared_pe(b):
                wait(pe, s_lo_done, count(b, 1, 1))
                if isinstance(b, int):
                    pe.wait_ge(s_w_lo, 2)
                for m in range(MI):
                    wait(pe, s_act_done, count(b, MI))
                    for n in range(2):
                        col = slice(n * FI + m * P, n * FI + (m + 1) * P)
                        for k in range(KT):
                            last = three(ps[:, 2 * m + n, :], sgu_hi[:, k, col], sgu_lo[:, k, col],
                                         s_hi[:, :, k, :], s_lo[:, :, k, :], k == 0, k == KT - 1)
                        last.then_inc(s_up_ready, 1)
                wait(pe, a_lo_done, count(b, MI, MI))
                for t in range(TT):
                    wait(pe, scaled_done, count(b, TT, t + 1 - TT))
                    for m in range(MI):
                        last = three(ps[:, 4 + t, :], a_hi[:, m, t * P:(t + 1) * P], a_lo[:, m, t * P:(t + 1) * P],
                                     swd_hi[:, m, :], swd_lo[:, m, :], m == 0, m == MI - 1)
                    last.then_inc(s_down_ready, 1)

            shared_pe(0)
            pe.wait_ge(mask_ready, 1)
            nc.tensor.matmul(ps[:, 0, :], tri[:, :], mask[:, :], start=True, stop=True)
            nc.tensor.matmul(ps[:, 1, :], ones_b[:, :], mask[:, :], start=True, stop=True).then_inc(rank_ready, 1)
            pe.wait_ge(slots_ready, 1)
            with pe.Fori(1, NB) as reg:
                shared_pe(reg)
            pe.wait_ge(s_act_done, NB * MI)
            for n in range(2 * NT):
                pe.wait_ge(hot_lo_done, 2 * (n + 1))
                nc.tensor.matmul(ps[:, 0, 0:NST], hot_lo[:, n % 2, :], hot_hi[:, n % 2, :],
                                 start=n == 0, stop=n == 2 * NT - 1).then_inc(hot_used, 1)
            phase_over(pe, 2)

            pe.sem_inc(y_ready, 1)

            def x_transposed(c, i):
                wait(pe, rows_in[c], count(i, 16, 16))
                wait(pe, xt_copied, count(i, RING, c - 1))
                for k in range(KT):
                    last = nc.tensor.transpose(ps[:, c % 2, k * P:(k + 1) * P], xg[:, c, k * P:(k + 1) * P],
                                               ident[:, :])
                last.then_inc(xt_ready, 1)

            def weights(i, c):
                n = slice(c + RING * i, c + RING * i + 1) if isinstance(i, int) else bass.ds(i * RING + c, 1)
                return (pe.value_load(need_i[0:1, n], min_val=1, max_val=NE),
                        pe.value_load(woff_i[0:1, n], min_val=0, max_val=(WSLOTS - 1) * WLEN))

            def down(c, i, woff):
                wait(pe, innerT_copied, count(i, RING, c + 1))
                wait(pe, y_copied, count(i, RING, c - 1))
                for m in range(MI):
                    last = nc.tensor.matmul(ps[:, 6 + c % 2, :], innerT[:, c % 2, m, :],
                                            wslots[:, bass.ds(woff + (KT * 2 * FI + m * D), D)],
                                            start=m == 0, stop=m == MI - 1)
                last.then_inc(y_ready, 1)

            def routed_pe(i, last_one=False):
                for c in range(RING):
                    if c + 1 < RING:
                        x_transposed(c + 1, i)
                    elif not last_one:
                        x_transposed(0, i + 1)
                    need, woff = weights(i, c)
                    pe.wait_ge(weights_ready, need)
                    wait(pe, xt_copied, count(i, RING, c + 1))
                    wait(pe, inner_done, count(i, RING, c - 1))
                    for k in range(KT):
                        last = nc.tensor.matmul(ps[:, 2 + c % 2, :], xT[:, c % 2, k, :],
                                                wslots[:, bass.ds(woff + k * 2 * FI, 2 * FI)],
                                                start=k == 0, stop=k == KT - 1)
                    last.then_inc(gu_ready, 1)
                    if c or not (isinstance(i, int) and i == 0):
                        pc, pi = (c - 1, i) if c else (RING - 1, i - 1)
                        down(pc, pi, weights(pi, pc)[1])
                    wait(pe, inner_done, count(i, RING, c + 1))
                    wait(pe, innerT_copied, count(i, RING, c - 1))
                    for m in range(MI):
                        last = nc.tensor.transpose(ps[:, 4 + c % 2, m * P:(m + 1) * P],
                                                   inner[:, c % 2, m * P:(m + 1) * P], ident[:, :])
                    last.then_inc(innerT_ready, 1)

            x_transposed(0, 0)
            routed_pe(0)
            with pe.Fori(1, NST // RING - 1) as reg:
                routed_pe(reg)
            routed_pe(NST // RING - 1, last_one=True)
            down(RING - 1, NST // RING - 1, weights(NST // RING - 1, RING - 1)[1])
            phase_over(pe, 3)


def kernel(**inputs):
    import numpy as np
    import concourse.bacc as bacc
    from concourse import mybir
    from concourse.bass_utils import run_bass_kernel_spmd

    def given(name):
        return np.asarray(inputs["L0_" + name])

    arrays = {
        "x": given("attn_x"), "wqkvT": given("attn_w_qkv").T, "woutT": given("attn_w_out").T,
        "b_out": given("attn_b_out"), "wrT": given("ffn_Wr").T, "r_bias": given("ffn_bias"),
        "Wg": given("ffn_Wg"), "Wu": given("ffn_Wu"), "Wd": given("ffn_Wd"),
        "sWg": given("ffn_sWg"), "sWu": given("ffn_sWu"), "sWd": given("ffn_sWd"),
        "cT": given("c").T, "wmod": given("wmod"),
    }
    arrays = {f"in_{name}_dram": np.ascontiguousarray(a) for name, a in arrays.items()}
    nc = bacc.Bacc("TRN2", target_bir_lowering=False, num_devices=1)
    args = [nc.dram_tensor(name, a.shape, mybir.dt.from_np(a.dtype), kind="ExternalInput").ap()
            for name, a in arrays.items()]
    x = arrays["in_x_dram"]
    out = nc.dram_tensor("out_0_dram", x.shape, mybir.dt.from_np(x.dtype), kind="ExternalOutput").ap()
    adaln_moe_block_kernel(nc, *args, out)
    r = run_bass_kernel_spmd(nc, [arrays], core_ids=[0])
    return r.results[0]["out_0_dram"]
```

```python
import concourse.bass as bass
from concourse import mybir
from contextlib import ExitStack


def adaln_moe_block_kernel(nc, x, wqkvT, woutT, b_out, wrT, r_bias, Wg, Wu, Wd, sWg, sWu, sWd, cT, wmod, out):
    f32 = mybir.dt.float32
    f32r = mybir.dt.float32r
    i32 = mybir.dt.int32
    ALU = mybir.AluOpType
    ACT = mybir.ActivationFunctionType
    AX = mybir.AxisListType

    NB, SEQ, D = x.shape
    P = 128
    KT = D // P
    TT = SEQ // P
    NT = NB * TT
    H = 16
    HD = D // H
    HG = P // HD
    NG = H // HG
    SCALE = 1.0 / float(HD) ** 0.5
    EPS = 1e-5
    NE = Wg.shape[0]
    FI = Wg.shape[2]
    MI = FI // P
    U = NG * TT * HG
    UG = TT * HG
    GA, GAB, CB1, SB, GB = range(5)
    NMOD = 5

    NST = 2 * NT + NE
    WSLOTS = 4
    WLEN = KT * 2 * FI + MI * D

    mod_d = nc.dram_tensor("mod_rows", (NMOD, NB, D), f32).ap()
    x1_d = nc.dram_tensor("x1_rows", (NT, P, D), f32).ap()
    h2_d = nc.dram_tensor("h2_rows", (NT * P, D), f32).ap()
    h2T_d = nc.dram_tensor("h2_transposed", (NB, TT, P, KT * P), f32).ap()
    y_d = nc.dram_tensor("routed_rows", (NST * P, D), f32).ap()

    x_t = x.rearrange("b (t p) d -> b p t d", p=P)
    x_tile = x.rearrange("b (t p) d -> (b t) p d", p=P)
    out_tile = out.rearrange("b (t p) d -> (b t) p d", p=P)
    wqkv_v = wqkvT.rearrange("(k p) n -> p k n", p=P)
    wout_v = woutT.rearrange("(k p) n -> p k n", p=P)
    wr_v = wrT.rearrange("(k p) n -> p k n", p=P)
    wmod_v = wmod.rearrange("(k p) n -> p k n", p=P)
    cT_v = cT.rearrange("(k p) n -> p k n", p=P)
    Wg_v = Wg.rearrange("e (k p) i -> e p k i", p=P)
    Wu_v = Wu.rearrange("e (k p) i -> e p k i", p=P)
    Wd_v = Wd.rearrange("e (m p) d -> e p m d", p=P)

    BODY = ([(1, 1, "ot", -2), (5, 5, "ot", -1)] + [(4 * t + 9, 4 * t + 9, "ot", t) for t in range(14)]
            + [(5 + 3 * t, 7 + 3 * t, "out", t) for t in range(TT)]
            + [(15, 15, "tr", 0), (23, 23, "tr", 1), (39, 39, "tr", 2), (47, 47, "tr", 3)]
            + [(19, 19, "route", 0), (27, 27, "route", 1), (43, 43, "route", 2), (51, 51, "route", 3)]
            + [(17, 18, "q", 2), (19, 21, "k", 2), (22, 25, "q", 3), (26, 29, "k", 3)]
            + [(30 + k, 30 + k, "ht", k) for k in range(KT)]
            + [(34, 37, "v", 0), (38, 41, "v", 1), (42, 44, "v", 2), (45, 47, "v", 3)]
            + [(48, 51, "q", 0), (52, 55, "k", 0), (56, 59, "q", 1), (60, 62, "k", 1)])
    TAIL = ([(1, 1, "ot", -2), (5, 5, "ot", -1)] + [(6 + 3 * t, 7 + 3 * t, "out", t) for t in range(TT)]
            + [(13 + 3 * t, 13 + 3 * t, "tr", t) for t in range(TT)]
            + [(15 + 3 * t, 15 + 3 * t, "route", t) for t in range(TT)])
    TAIL_END = 28
    OF_PREV = ("out", "tr", "route")
    TURNS = {"long": (0, 1), "short": (2,)}
    CLASS = dict(out="long", q="long", k="long", v="long", mod="long", ht="long",
                 modT="short", tr="short", ot="short", route="short")
    BODY.sort(key=lambda w: w[1])
    TAIL.sort(key=lambda w: w[1])

    def of_next(kind, i):
        return kind in ("ht", "v") or (kind in "qk" and i < 2)

    def runs(kind, i, b):
        return b is None or not ((b == 0 and (kind in OF_PREV or i < 0)) or (b == NB - 1 and of_next(kind, i)))

    PRO = ([("modT", 0)] + [("ht", k) for k in range(KT)] + [("q", 0), ("k", 0), ("mod", 0), ("mod", 1)]
           + [("v", t) for t in range(TT)] + [("q", 1), ("k", 1), ("mod", 2), ("mod", 3)])
    dense_order = [(-1, k, i) for k, i in PRO]
    for _b in range(NB):
        dense_order += [(_b, k, i) for _, _, k, i in BODY if runs(k, i, _b)]
    dense_order += [(NB, k, i) for _, _, k, i in TAIL]
    of_class = {c: [(k, i) for _, _, k, i in BODY if CLASS[k] == c] for c in TURNS}
    per_place = {p: len(of_class[c]) // len(TURNS[c]) for c in TURNS for p in TURNS[c]}
    place = {}
    used = [0] * 3
    came = dict.fromkeys(TURNS, 0)
    for _b, _k, _i in dense_order:
        _c = CLASS[_k]
        turn = of_class[_c].index((_k, _i)) if 0 <= _b < NB else came[_c]
        bank = TURNS[_c][turn % len(TURNS[_c])]
        place[(_b, _k, _i)] = (bank, came[_c], used[bank])
        used[bank] += 1
        came[_c] += 1

    class Batch:

        def __init__(self, at, reg=None):
            self.at, self.reg = at, reg

        @property
        def side(self):
            return self.at % 2

        def lin(self, per, off):
            return 2 * per * self.reg + (per * self.at + off) if self.reg is not None else per * self.at + off

        def dense(self, kind, i, back=0):
            if self.reg is None:
                return place[(self.at - back, kind, i)]
            bank, n, uses = place[(1, kind, i)]
            n_body = len(of_class[CLASS[kind]])
            return (bank, self.lin(n_body, n - (1 + back) * n_body),
                    self.lin(per_place[bank], uses - (1 + back) * per_place[bank]))

        def has(self, kind, i):
            return runs(kind, i, None if self.reg is not None else self.at)

        @property
        def first(self):
            return self.reg is None and self.at == 0

        @property
        def last(self):
            return self.reg is None and self.at == NB - 1

        @property
        def after_last(self):
            return self.reg is None and self.at == NB

        def table(self):
            return TAIL if self.after_last else [w for w in BODY if self.has(w[2], w[3])]

        def work(self, u, lag=0):
            return [(k, i) for _, end, k, i in self.table() if end == u - lag]

        def parts(self, u):
            got = []
            for start, end, kind, i in self.table():
                ks = [k for k in range(KT) if start + k * (end - start + 1) // KT == u]
                if ks:
                    got.append((kind, i, ks))
            return got

    def wait(eng, sem, value):
        if not isinstance(value, int) or value > 0:
            eng.wait_ge(sem, value)

    VW = HD + 1
    GAP_MAX = 85.0

    def before(b, u, lag):
        return (u < lag or not b.after_last) and (u >= lag or not b.first)

    ctx = ExitStack()
    with ctx:
        def sb(name, shape, dt=f32):
            return ctx.enter_context(nc.sbuf_tensor(name, shape, dt))

        def sem(name):
            return ctx.enter_context(nc.semaphore(name))

        ps = ctx.enter_context(nc.psum_tensor("ps", [P, 8, 512], f32))
        S_BANK, PT_BANK, AV_BANK, D_BANK = 0, 2, 3, 5

        ident = sb("ident", [P, P])
        wr_hi = sb("wr_hi", [P, KT, NE], f32r)
        wr_lo = sb("wr_lo", [P, KT, NE], f32r)
        wr_raw = sb("wr_raw", [P, KT, NE])
        scT = sb("silu_c", [P, KT, NB])
        modT = sb("sa_ca_columns", [P, 2, KT, NB])
        rbias = sb("router_bias", [P, NE])
        logits = sb("logits", [P, NT, NE])

        one = ExitStack()

        def sb1(name, shape, dt=f32):
            return one.enter_context(nc.sbuf_tensor(name, shape, dt))

        wqkv_hi = sb1("wqkv_hi", [P, KT, 3 * D], f32r)
        wqkv_lo = sb1("wqkv_lo", [P, KT, 3 * D], f32r)
        wout_hi = sb1("wout_hi", [P, KT, D], f32r)
        wout_lo = sb1("wout_lo", [P, KT, D], f32r)
        hT_hi = sb1("hT_hi", [P, KT, SEQ], f32r)
        hT_lo = sb1("hT_lo", [P, KT, SEQ], f32r)
        ht_full = sb1("ht_full", [P, SEQ])
        xnat = sb1("xnat", [P, TT, D])
        half_hi = sb1("half_hi", [P, 2, SEQ], f32r)
        half_lo = sb1("half_lo", [P, 2, SEQ], f32r)
        qstack = sb1("qstack", [P, 2, HG, SEQ], f32r)
        kstack = sb1("kstack", [P, 2, HG, SEQ], f32r)
        V = sb1("V", [P, 2, TT, H * VW])
        probs = sb1("probs", [P, 2, SEQ])
        probsT = sb1("probsT", [P, 2, TT, P])
        tile_rows = sb1("tile_rows", [P, 2, TT, HG, HD])
        neg_max = sb1("neg_max", [P, 4, TT])
        neg_top = sb1("neg_top", [P, 4])
        gap = sb1("gap", [P, 4, TT])
        inv = sb1("inv", [P, 4, TT])
        weighed = sb1("weighed", [P, 2, TT])
        total = sb1("total", [P, 2])
        factor = sb1("factor", [P, 2, TT])
        outT_hi = sb1("outT_hi", [P, NG, SEQ], f32r)
        outT_lo = sb1("outT_lo", [P, NG, SEQ], f32r)
        post = sb1("post", [P, 4, D])
        h2 = sb1("h2", [P, TT, D])
        h2T = ht_full[:, :].rearrange("p (k n) -> p k n", k=KT)
        h2T_hi = sb1("h2T_hi", [P, KT, P], f32r)
        h2T_lo = sb1("h2T_lo", [P, KT, P], f32r)
        bc = sb1("bc", [P, 4, D])
        stats1 = sb1("stats1", [P, TT, 6])
        mv1 = sb1("mv1", [P, TT, 2])
        rstd1 = sb1("rstd1", [P, TT])
        minus_half = sb1("minus_half", [P, TT])
        stats2 = sb1("stats2", [P, 2, 6])
        mv2 = sb1("mv2", [P, 2, 2])
        rstd2 = sb1("rstd2", [P, 2])

        one.close()

        base = sb("base", [P, NT, D])
        wslots = sb("wslots", [P, WSLOTS * WLEN])
        wts = sb("token_weights", [P, 2, NT])
        slot_i = sb("slot_i", [P, 2, NT], i32)
        gather_i = sb("gather_i", [P, NST], i32)
        need_i = sb("need_i", [1, NST], i32)
        woff_i = sb("woff_i", [1, NST], i32)
        freed_i = sb("freed_i", [1, NE], i32)
        three_ = ExitStack()

        def sb3(name, shape, dt=f32):
            return three_.enter_context(nc.sbuf_tensor(name, shape, dt))

        sgu_hi = sb3("sgu_hi", [P, KT, 2 * FI], f32r)
        sgu_lo = sb3("sgu_lo", [P, KT, 2 * FI], f32r)
        swd_hi = sb3("swd_hi", [P, MI, D], f32r)
        swd_lo = sb3("swd_lo", [P, MI, D], f32r)
        s_raw = sb3("s_raw", [P, TT, KT, P])
        s_hi = sb3("s_hi", [P, TT, KT, P], f32r)
        s_lo = sb3("s_lo", [P, TT, KT, P], f32r)
        s_gate = sb3("s_gate", [P, MI, SEQ])
        s_act = sb3("s_act", [P, MI, SEQ])
        a_hi = sb3("a_hi", [P, MI, SEQ], f32r)
        a_lo = sb3("a_lo", [P, MI, SEQ], f32r)
        gbrow = sb3("gbrow", [P, D])
        scaled = sb3("scaled", [P, 2, D])
        sgu_raw = base[:, NT - 8:NT - 4, :]
        swd_raw = base[:, NT - 4:NT - 4 + MI, :]

        r_at = [2 * WLEN]

        def rt(n, dt=f32):
            r_at[0] += n
            assert r_at[0] <= WSLOTS * WLEN
            v = wslots[:, r_at[0] - n:r_at[0]]
            return v if dt == f32 else v.bitcast(dt)

        TE = NT * NE
        prob = rt(TE)
        eq = rt(TE)
        order = rt(TE)
        oh = [rt(TE), rt(TE)]
        tot_e = rt(TE)
        run = rt(TE)
        slot_of = rt(TE)
        ones_te = rt(TE)
        iota_e = rt(NE)
        iota_t = rt(NST)
        row_max, row_sum = rt(NT), rt(NT)
        top = [rt(NT), rt(NT)]
        first = rt(NT)
        den = rt(NT)
        cnt = rt(NE)
        cum_prev = rt(NE)
        tiles_i = rt(NE, i32)
        tiles = rt(NE)
        tiles_cum = rt(NE)
        offset = rt(NE)
        slots = rt(2 * NT)
        slots_hi, slots_lo = rt(2 * NT), rt(2 * NT)
        tmp_i = rt(2 * NT, i32)
        tmp2_i = rt(2 * NT, i32)
        e_tab = rt(NST)
        e_tab_i = rt(NST, i32)
        tokid = rt(NT)
        tri = sb3("tri", [P, P], mybir.dt.bfloat16)
        ones_b = sb3("ones_b", [P, P], mybir.dt.bfloat16)
        mask = sb3("mask", [P, TE], mybir.dt.bfloat16)
        iota_p = sb3("iota_p", [P, P])
        HOTS = 4
        hot_lo = sb3("hot_lo", [P, 2, HOTS, P], f32r)
        hot_hi = sb3("hot_hi", [P, 2, HOTS, NST], f32r)
        hot_at = sb3("hot_at", [P, HOTS, NST])
        three_.close()

        four = ExitStack()

        def sb4(name, shape, dt=f32):
            return four.enter_context(nc.sbuf_tensor(name, shape, dt))

        RING = 4
        xg = sb4("xg", [P, RING, D])
        xT = sb4("xT", [P, 2, KT, P])
        gate = sb4("gate", [P, 2, FI])
        inner = sb4("inner", [P, 2, FI])
        innerT = sb4("innerT", [P, 2, MI, P])
        yrow = sb4("yrow", [P, RING, D])
        gidx = sb4("gidx", [P, RING], i32)
        four.close()
        five = ExitStack()
        rows0 = five.enter_context(nc.sbuf_tensor("rows0", [P, 2, TT, D], f32))
        rows1 = five.enter_context(nc.sbuf_tensor("rows1", [P, 2, TT, D], f32))
        gb2 = five.enter_context(nc.sbuf_tensor("gb2", [P, 2, D], f32))
        ridx = five.enter_context(nc.sbuf_tensor("ridx", [P, 2, 2, TT], i32))
        five.close()
        identity_ready = sem("identity_ready")
        const_in = sem("const_in")
        silu_c_ready = sem("silu_c_ready")
        chunk_in = [sem("chunk_in0"), sem("chunk_in1")]
        w_hi_done = sem("w_hi_done")
        w_lo_done = sem("w_lo_done")
        row_step = sem("row_step")
        gate_step = sem("gate_step")
        row_out = sem("row_out")
        x_in = sem("x_in")
        ln1_step = sem("ln1_step")
        rstd1_step = sem("rstd1_step")
        xn_done = sem("xn_done")
        ht_hi_done = sem("ht_hi_done")
        ht_lo_done = sem("ht_lo_done")
        long_ready = sem("long_ready")
        short_ready = sem("short_ready")
        dense_free = [sem(f"dense_free{n}") for n in range(3)]
        ones_ready = sem("ones_ready")
        half_hi_done = sem("half_hi_done")
        q_stacked = sem("q_stacked")
        k_stacked = sem("k_stacked")
        scores_ready = sem("scores_ready")
        max_ready = sem("max_ready")
        exp_done = sem("exp_done")
        block_max_done = sem("block_max_done")
        gap_ready = sem("gap_ready")
        inv_ready = sem("inv_ready")
        factor_step = sem("factor_step")
        pair_done = sem("pair_done")
        tile_step = sem("tile_step")
        pt_ready = sem("pt_ready")
        pt_free = sem("pt_free")
        av_done = sem("av_done")
        out_hi_done = sem("out_hi_done")
        bc_in = sem("bc_in")
        xr_in = [sem("xr_in0"), sem("xr_in1")]
        xb_done = sem("xb_done")
        x1_done = sem("x1_done")
        x1_out = [sem("x1_out0"), sem("x1_out1")]
        ln2_step = sem("ln2_step")
        rstd2_step = sem("rstd2_step")
        h2_normal = sem("h2_normal")
        h2_step = sem("h2_step")
        h2_out = sem("h2_out")
        tr_lo_done = sem("tr_lo_done")
        h2T_out = sem("h2T_out")
        phase_end = sem("phase_end")
        passed_pool = sem("passed_pool")
        passed_dve = sem("passed_dve")
        passed_sp = sem("passed_sp")

        def wait_apart(eng, sem, value, passed):
            wait(eng, sem, value)
            if not isinstance(value, int):
                eng.sem_inc(passed, 1)
        s_w_in = sem("s_w_in")
        s_w_hi = sem("s_w_hi")
        s_w_lo = sem("s_w_lo")
        s_in = sem("s_in")
        s_x1_in = sem("s_x1_in")
        s_gb_in = sem("s_gb_in")
        s_hi_done = sem("s_hi_done")
        s_lo_v = sem("s_lo_v")
        s_lo_p = sem("s_lo_p")
        s_up_ready = sem("s_up_ready")
        s_gate_done = sem("s_gate_done")
        s_act_done = sem("s_act_done")
        a_hi_done = sem("a_hi_done")
        a_lo_done = sem("a_lo_done")
        s_down_ready = sem("s_down_ready")
        scaled_done = sem("scaled_done")
        base_done = sem("base_done")
        r_const = sem("r_const")
        r_step = sem("r_step")
        r_exp = sem("r_exp")
        mask_ready = sem("mask_ready")
        rank_ready = sem("rank_ready")
        slots_ready = sem("slots_ready")
        hot_step = sem("hot_step")
        hot_done = sem("hot_done")
        hot_used = sem("hot_used")
        weights_in = [sem("weights_in0"), sem("weights_in1")]
        weights_ready = sem("weights_ready")
        gidx_done = sem("gidx_done")
        rows_in = [sem(f"rows_in{n}") for n in range(4)]
        xt_ready = sem("xt_ready")
        xt_copied = sem("xt_copied")
        gu_ready = sem("gu_ready")
        gate_done = sem("gate_done")
        inner_done = sem("inner_done")
        innerT_ready = sem("innerT_ready")
        innerT_copied = sem("innerT_copied")
        y_ready = sem("y_ready")
        y_copied = sem("y_copied")
        y_out = [sem(f"y_out{n}") for n in range(4)]
        ridx_done = sem("ridx_done")
        pair_in = [[sem(f"pair_in{side}_{t}") for t in range(TT)] for side in range(2)]
        gb2_in = [sem(f"gb2_in{side}") for side in range(2)]
        first_scaled = sem("first_scaled")
        pair_added = sem("pair_added")
        gated_v = sem("gated_v")
        gated_p = sem("gated_p")
        result_done = sem("result_done")
        result_out = [[sem(f"result_out{side}_{t}") for t in range(TT)] for side in range(2)]

        stage = [h2[:, :, :], post[:, :, :]]
        CHUNKS = [("modT", 0), ("modT", 1), ("w", 0), ("w", 1), ("w", 2),
                  ("mod", 0), ("mod", 1), ("mod", 2), ("mod", 3), ("w", 3)]
        MOD_COLS = [2, 4, 3, 5]
        MOD_ROW = [GA, CB1, SB, GB]

        def batches(eng, body):
            body(Batch(0))
            body(Batch(1))
            with eng.Fori(1, NB // 2 - 1) as reg:
                body(Batch(0, reg))
                body(Batch(1, reg))
            body(Batch(NB - 2))
            body(Batch(NB - 1))
            body(Batch(NB))

        def ready(kind):
            return {"long": long_ready, "short": short_ready}[CLASS[kind]]

        def values(side, t):
            return V[:, side, t, :].rearrange("p (h c) -> p h c", c=VW)[:, :, 0:HD]

        ENGINES = 5

        def phase_over(eng, n):
            eng.drain().then_inc(phase_end, 1)
            eng.wait_ge(phase_end, ENGINES * n)

        def each_batch(eng, body):
            body(0)
            with eng.Fori(1, NB) as reg:
                body(reg)

        def each_pair(eng, body):
            body(0, 0, 0)
            body(1, 1, 0)
            with eng.Fori(1, NB // 2) as reg:
                body(2 * reg, 0, reg)
                body(2 * reg + 1, 1, reg)

        def count(b, per=1, off=0):
            return b * per + off

        def dyn(ap, first_dim, n):
            return ap[n] if isinstance(n, int) else ap[bass.ds(n, 1)].rearrange(first_dim)

        block = ctx.enter_context(nc.Block())

        @block.sync
        def _(sp):
            sp.dma_start(scT[:, :, :], cT_v).then_inc(const_in, 16)
            sp.dma_start(wr_raw[:, :, :], wr_v).then_inc(const_in, 16)
            sp.dma_start(rbias[:, :], r_bias.partition_broadcast(P)).then_inc(const_in, 16)
            sp.dma_start(V[0:NB, 1, 3, 0:D], b_out.partition_broadcast(NB)).then_inc(const_in, 16)

            def chunk(c):
                kind, i = CHUNKS[c]
                if c >= 2:
                    k0, i0 = CHUNKS[c - 2]
                    if k0 == "w":
                        sp.wait_ge(w_hi_done, i0 + 1)
                        sp.wait_ge(w_lo_done, i0 + 1)
                    else:
                        sp.wait_ge(ready(k0), place[(-1, k0, i0 if k0 == "mod" else 0)][1] + 1)
                src = (wmod_v[:, :, i * D:(i + 1) * D] if kind == "modT" else
                       wmod_v[:, :, MOD_COLS[i] * D:(MOD_COLS[i] + 1) * D] if kind == "mod" else
                       wqkv_v[:, :, i * D:(i + 1) * D] if i < 3 else wout_v)
                sp.dma_start(stage[c % 2], src).then_inc(chunk_in[c % 2], 16)

            chunk(0)
            chunk(1)
            sp.dma_start(xnat[:, :, :], x_t[0]).then_inc(x_in, 16)
            for c in range(2, 7):
                chunk(c)
            def stack(b, kind, i):
                which, dst, done = (0, qstack, q_stacked) if kind == "q" else (1, kstack, k_stacked)
                if b is None:
                    bank, _, uses = place[(-1, kind, i)]
                    wait(sp, dense_free[bank], uses + 1)
                else:
                    bank, _, uses = b.dense(kind, i)
                    g = i if i > 1 else i + NG
                    wait_apart(sp, dense_free[bank], uses + 1, passed_sp)
                    wait(sp, scores_ready, b.lin(U, UG * (g - 1)))
                for r in range(4):
                    half = half_lo if r in ((1, 3) if kind == "q" else (2, 3)) else half_hi
                    for j in range(HG):
                        sp.dma_start(dst[HD * r:HD * r + HD, i % 2, j, :].bitcast(f32),
                                     half[HD * j:HD * j + HD, which, :].bitcast(f32)).then_inc(done, 16)

            stack(None, "q", 0)
            chunk(7)
            stack(None, "k", 0)
            stack(None, "q", 1)
            stack(None, "k", 1)
            chunk(8)
            chunk(9)
            for m, n in enumerate((2, 3, 4, 5)):
                sp.wait_ge(row_step, n)
                sp.dma_start(mod_d[MOD_ROW[m]], bc[0:NB, m, :]).then_inc(row_out, 16)
                if m == 0:
                    sp.dma_start(mod_d[GAB], V[0:NB, 1, 2, 0:D]).then_inc(row_out, 16)
            sp.wait_ge(row_out, 16 * NMOD)
            sp.wait_ge(long_ready, place[(-1, "ht", KT - 1)][1] + 1)
            sp.dma_start(xnat[:, :, :], x_t[1]).then_inc(x_in, 16)

            def body(b):
                def tile(t, back=1):
                    return b.lin(TT, t - back * TT)

                def load_x_again(t, back=1):
                    wait(sp, x1_done, b.lin(TT, max(t - 1, 0) - back * TT))
                    src = x_tile[tile(t, back)] if b.reg is None else \
                        x_tile[bass.ds(tile(t, back), 1)].rearrange("a p d -> p (a d)")
                    sp.dma_start(post[:, t % 2, :], src).then_inc(xr_in[t % 2], 16)

                for u in range(TAIL_END if b.after_last else U):
                    if u == 2 * UG and not b.after_last:
                        stack(b, "q", NG - 1)
                        stack(b, "k", NG - 1)
                    if u == 42 and not b.after_last and (b.reg is not None or b.at < NB - 2):
                        wait(sp, long_ready, b.dense("ht", KT - 1)[1] + 1)
                        sp.dma_start(xnat[:, :, :], x_t[b.at + 2] if b.reg is None else
                                     x_t[bass.ds(b.lin(1, 2), 1)].rearrange("a p t d -> p (a t) d"))\
                            .then_inc(x_in, 16)
                    if u == 48 and not b.after_last:
                        wait(sp, h2_step, b.lin(2 * TT, 0))
                        for n, m in enumerate((GA, GAB, CB1, SB)):
                            if b.reg is None:
                                row = mod_d[m, b.at].partition_broadcast(P)
                            else:
                                row = mod_d[m, bass.ds(b.lin(1, 0), 1)].rearrange("a d -> (a d)")\
                                    .partition_broadcast(P)
                            sp.dma_start(bc[:, n, :], row).then_inc(bc_in, 16)
                        load_x_again(0, 0)
                        load_x_again(1, 0)
                    for kind, i in b.work(u, 1):
                        if kind in "qk" and i != NG - 1:
                            stack(b, kind, i)
                        if kind == "tr":
                            bank, _, uses = b.dense(kind, i)
                            wait(sp, dense_free[bank], uses + 1)
                            dst = h2T_d[b.at - 1, i] if b.reg is None else \
                                h2T_d[bass.ds(b.lin(1, -1), 1), i].rearrange("a p n -> p (a n)")
                            sp.dma_start(dst, h2T[:, :, :].rearrange("p k n -> p (k n)")).then_inc(h2T_out, 16)
                    for kind, i in b.work(u, 2):
                        if kind == "out":
                            wait(sp, x1_done, b.lin(TT, i - TT + 1))
                            dst = x1_d[tile(i)] if b.reg is None else \
                                x1_d[bass.ds(tile(i), 1)].rearrange("a p d -> p (a d)")
                            sp.dma_start(dst, post[:, 2 + i % 2, :]).then_inc(x1_out[i % 2], 16)
                            if i + 2 < TT:
                                load_x_again(i + 2)
                    for kind, i in b.work(u, 6):
                        if kind == "out":
                            wait(sp, h2_step, b.lin(2 * TT, 2 * (i - TT + 1)))
                            dst = h2_d[P * tile(i):P * tile(i) + P] if b.reg is None else \
                                h2_d[bass.ds(P * tile(i), P)]
                            sp.dma_start(dst, h2[:, i, :]).then_inc(h2_out, 16)

            batches(sp, body)
            sp.wait_ge(h2T_out, 16 * NT)
            sp.wait_ge(h2_out, 16 * NT)
            for n in range(2):
                sp.wait_ge(x1_out[n], 16 * NT // 2)
            phase_over(sp, 1)

            sp.dma_start(sgu_raw[:, :, 0:FI], sWg.rearrange("(k p) i -> p k i", p=P)).then_inc(s_w_in, 16)
            sp.dma_start(sgu_raw[:, :, FI:], sWu.rearrange("(k p) i -> p k i", p=P)).then_inc(s_w_in, 16)
            sp.dma_start(swd_raw, sWd.rearrange("(m p) d -> p m d", p=P)).then_inc(s_w_in, 16)

            def load_expert(e):
                o = e % WSLOTS * WLEN
                gu = wslots[:, o:o + KT * 2 * FI].rearrange("p (k n) -> p k n", k=KT)
                dn = wslots[:, o + KT * 2 * FI:o + WLEN].rearrange("p (m d) -> p m d", m=MI)
                for dst, src in ((gu[:, :, 0:FI], Wg_v[e]), (gu[:, :, FI:], Wu_v[e]), (dn, Wd_v[e])):
                    sp.dma_start(dst, src).then_inc(weights_in[e % 2], 16)

            def shared_loads(b):
                wait(sp, s_hi_done, count(b))
                wait(sp, s_lo_v, count(b))
                wait(sp, s_lo_p, count(b))
                src = h2T_d[b] if isinstance(b, int) else h2T_d[bass.ds(b, 1)].rearrange("a t p n -> (a t) p n")
                sp.dma_start(s_raw[:, :, :, :].rearrange("p t k n -> p t (k n)"),
                             src.rearrange("t p n -> p t n")).then_inc(s_in, 16)
                wait(sp, scaled_done, count(b, TT))
                row = mod_d[GB, b] if isinstance(b, int) else mod_d[GB, bass.ds(b, 1)].rearrange("a d -> (a d)")
                sp.dma_start(gbrow[:, :], row.partition_broadcast(P)).then_inc(s_gb_in, 16)
                if isinstance(b, int):
                    sp.wait_ge(s_w_lo, 2)
                sp.dma_start(base[:, bass.ds(b * TT, TT), :] if not isinstance(b, int) else
                             base[:, b * TT:(b + 1) * TT, :],
                             (x1_d[bass.ds(b * TT, TT)] if not isinstance(b, int) else
                              x1_d[b * TT:(b + 1) * TT]).rearrange("t p d -> p t d")).then_inc(s_x1_in, 16)
                if isinstance(b, int):
                    load_expert(0)
                    load_expert(1)

            each_batch(sp, shared_loads)
            phase_over(sp, 2)

            def loaded(e):
                sp.wait_ge(weights_in[e % 2], 48 * (e // 2 + 1))
                sp.sem_inc(weights_ready, 1)

            for e in range(2, NE):
                if e >= WSLOTS:
                    done = sp.value_load(freed_i[0:1, e - WSLOTS:e - WSLOTS + 1], min_val=1, max_val=NST + 1)
                    wait_apart(sp, y_ready, done, passed_sp)
                loaded(e - 2)
                load_expert(e)
            loaded(NE - 2)
            loaded(NE - 1)
            phase_over(sp, 3)

            def load_gate(b, side):
                row = mod_d[GB, b] if isinstance(b, int) else mod_d[GB, bass.ds(b, 1)].rearrange("a d -> (a d)")
                sp.dma_start(gb2[:, side, :], row.partition_broadcast(P)).then_inc(gb2_in[side], 16)

            def combine_out(b, side, last=False):
                for t in range(TT):
                    wait(sp, result_done, count(b, TT, t + 1))
                    sp.dma_start(dyn(out_tile, "a p d -> p (a d)", b * TT + t), rows1[:, side, t, :])\
                        .then_inc(result_out[side][t], 16)
                if not last:
                    load_gate(b + 2, side)

            load_gate(0, 0)
            load_gate(1, 1)
            with sp.Fori(0, NB // 2 - 1) as reg:
                combine_out(2 * reg, 0)
                combine_out(2 * reg + 1, 1)
            combine_out(NB - 2, 0, last=True)
            combine_out(NB - 1, 1, last=True)
            for side in range(2):
                for t in range(TT):
                    sp.wait_ge(result_out[side][t], 16 * NB // 2)

        @block.gpsimd
        def _(pool):
            nc.gpsimd.memset(minus_half[:, :], -0.5)
            nc.gpsimd.memset(ident[:, :], 0.0).then_inc(identity_ready, 1)
            pool.wait_ge(identity_ready, 1)
            nc.gpsimd.affine_select(out=ident[:, :], in_=ident[:, :], compare_op=ALU.not_equal, fill=1.0,
                                    base=0, pattern=[[-1, P]], channel_multiplier=1).then_inc(identity_ready, 1)

            def rstd_1(n):
                wait_apart(pool, ln1_step, n * 2 * TT, passed_pool)
                nc.gpsimd.tensor_scalar(rstd1[:, :], mv1[:, :, 1], EPS, None, ALU.add).then_inc(rstd1_step, 1)
                wait(pool, rstd1_step, n * 2 - 1)
                nc.gpsimd.tensor_tensor(rstd1[:, :], rstd1[:, :], minus_half[:, :], ALU.pow)\
                    .then_inc(rstd1_step, 1)

            def ht_low(n, k):
                wait(pool, ht_hi_done, n + 1)
                nc.gpsimd.tensor_tensor(hT_lo[:, k, :], ht_full[:, :], hT_hi[:, k, :],
                                        ALU.subtract).then_inc(ht_lo_done, 1)

            values_of = V[:, 0, :, :].rearrange("p t (h c) -> p t h c", c=VW)
            nc.gpsimd.memset(values_of[:, :, :, HD:VW], 1.0).then_inc(ones_ready, 1)
            rstd_1(1)
            for k in range(KT):
                ht_low(k, k)
            pool.wait_ge(row_out, 16 * NMOD)
            values_of = V[:, 1, :, :].rearrange("p t (h c) -> p t h c", c=VW)
            nc.gpsimd.memset(values_of[:, :, :, HD:VW], 1.0).then_inc(ones_ready, 1)

            def body(b):
                for u in range(TAIL_END if b.after_last else U):
                    if u % HG == 3 and before(b, u, 7):
                        n = (u - 7) // HG
                        parts = tile_rows[:, n % 2, :, :, :]
                        wait(pool, pair_done, b.lin(U // 2, 2 * (n + 1)))
                        nc.gpsimd.tensor_tensor(parts[:, 0:2], parts[:, 0:2], parts[:, 2:4],
                                                ALU.add).then_inc(tile_step, 1)
                        wait(pool, tile_step, b.lin(2 * NG * TT, 2 * n + 1))
                        nc.gpsimd.tensor_tensor(parts[:, 0], parts[:, 0], parts[:, 1],
                                                ALU.add).then_inc(tile_step, 1)
                    for kind, i in b.work(u, 1):
                        if kind == "out":
                            wait(pool, xr_in[i % 2], b.lin(16 * TT // 2, 16 * (i // 2 + 1) - 16 * TT // 2))
                            if i == 0:
                                wait(pool, bc_in, b.lin(64, 0))
                            nc.gpsimd.tensor_tensor(post[:, i % 2, :], post[:, i % 2, :], bc[:, 1, :],
                                                    ALU.add).then_inc(xb_done, 1)
                            bank, _, uses = b.dense(kind, i)
                            wait(pool, dense_free[bank], uses + 1)
                            wait(pool, xb_done, b.lin(TT, i + 1 - TT))
                            nc.gpsimd.tensor_tensor(post[:, 2 + i % 2, :], post[:, 2 + i % 2, :],
                                                    post[:, i % 2, :], ALU.add).then_inc(x1_done, 1)
                        if kind == "tr":
                            bank, _, uses = b.dense(kind, i)
                            wait(pool, dense_free[bank], uses + 1)
                            nc.gpsimd.tensor_tensor(h2T_lo[:, :, :], h2T[:, :, :], h2T_hi[:, :, :],
                                                    ALU.subtract).then_inc(tr_lo_done, 1)
                        if kind == "ht":
                            ht_low(b.lin(KT, KT + i), i)
                    for kind, i in b.work(u, 3):
                        if kind == "out":
                            n2 = b.lin(2 * TT, 2 * (i - TT))
                            wait_apart(pool, ln2_step, n2 + 2, passed_pool)
                            rstd = rstd2[:, i % 2:i % 2 + 1]
                            nc.gpsimd.tensor_scalar(rstd, mv2[:, i % 2, 1:2], EPS, None, ALU.add)\
                                .then_inc(rstd2_step, 1)
                            wait(pool, rstd2_step, n2 + 1)
                            nc.gpsimd.tensor_tensor(rstd, rstd, minus_half[:, 0:1], ALU.pow)\
                                .then_inc(rstd2_step, 1)
                    for kind, i in b.work(u, 4):
                        if kind == "out":
                            n2 = b.lin(2 * TT, 2 * (i - TT))
                            wait(pool, h2_normal, b.lin(TT, i + 1 - TT))
                            nc.gpsimd.tensor_tensor(h2[:, i, :], h2[:, i, :], bc[:, 2, :],
                                                    ALU.mult).then_inc(h2_step, 1)
                            wait(pool, h2_step, n2 + 1)
                            nc.gpsimd.tensor_tensor(h2[:, i, :], h2[:, i, :], bc[:, 3, :],
                                                    ALU.add).then_inc(h2_step, 1)
                    if u == 23 and b.has("ht", 0) and not b.after_last:
                        rstd_1(b.lin(1, 2))

            batches(pool, body)
            phase_over(pool, 1)

            nc.gpsimd.memset(tri[:, :], 1.0).then_inc(r_const, 1)
            nc.gpsimd.memset(ones_b[:, :], 1.0).then_inc(r_const, 1)
            nc.gpsimd.memset(ones_te, 1.0).then_inc(r_const, 1)
            pool.wait_ge(r_const, 3)
            nc.gpsimd.affine_select(out=tri[:, :], in_=tri[:, :], compare_op=ALU.is_gt, fill=0.0, base=0,
                                    pattern=[[1, P]], channel_multiplier=-1).then_inc(r_const, 1)
            IMP = dict(allow_small_or_imprecise_dtypes=True)
            nc.gpsimd.iota(iota_e, [[1, NE]], base=0, channel_multiplier=0, **IMP).then_inc(r_const, 1)
            nc.gpsimd.iota(iota_t, [[1, NST]], base=0, channel_multiplier=0, **IMP).then_inc(r_const, 1)
            nc.gpsimd.iota(iota_p[:, :], [[1, P]], base=0, channel_multiplier=0, **IMP).then_inc(r_const, 1)
            nc.gpsimd.iota(tokid, [[P, NT]], base=0, channel_multiplier=1, **IMP).then_inc(r_const, 1)

            def half_low_rows(n):
                wait(pool, s_hi_done, n)
                nc.gpsimd.tensor_tensor(s_lo[:, TT // 2:, :, :], s_raw[:, TT // 2:, :, :],
                                        s_hi[:, TT // 2:, :, :], ALU.subtract).then_inc(s_lo_p, 1)

            def shared_low(b, last=False):
                for m in range(MI):
                    wait(pool, a_hi_done, count(b, MI, m + 1))
                    nc.gpsimd.tensor_tensor(a_lo[:, m, :], s_act[:, m, :], a_hi[:, m, :],
                                            ALU.subtract).then_inc(a_lo_done, 1)
                if not last:
                    half_low_rows(count(b, 1, 2))
                for t in range(TT):
                    wait(pool, scaled_done, count(b, TT, t + 1))
                    if t == 0:
                        wait(pool, s_x1_in, count(b, 16, 16))
                    row = base[:, b * TT + t, :] if isinstance(b, int) else \
                        base[:, bass.ds(b * TT + t, 1), :].rearrange("p a d -> p (a d)")
                    nc.gpsimd.tensor_tensor(row, row, scaled[:, t % 2, :], ALU.add).then_inc(base_done, 1)

            half_low_rows(1)
            shared_low(0, last=True)
            half_low_rows(2)
            with pool.Fori(1, NB - 1) as reg:
                shared_low(reg)
            shared_low(NB - 1, last=True)
            phase_over(pool, 2)

            def gather(i):
                for c in range(RING):
                    if not isinstance(i, int) or i > 0:
                        wait(pool, xt_ready, count(i, RING, c + 1 - RING))
                        wait(pool, rows_in[c], count(i, 16))
                    col = gather_i[:, c:c + 1] if isinstance(i, int) else gather_i[:, bass.ds(i * RING + c, 1)]
                    nc.gpsimd.tensor_copy(gidx[:, c:c + 1], col).then_inc(gidx_done, 1)
                    wait_apart(pool, gidx_done, count(i, RING, c + 1), passed_pool)
                    nc.gpsimd.indirect_dma_start(
                        out=xg[:, c, :], out_offset=None, in_=h2_d[:, :],
                        in_offset=bass.IndirectOffsetOnAxis(ap=gidx[:, c:c + 1], axis=0))\
                        .then_inc(rows_in[c], 16)

            gather(0)
            with pool.Fori(1, NST // RING) as reg:
                gather(reg)
            phase_over(pool, 3)

            def fetch(b, side, h):
                for t in range(TT):
                    wait_apart(pool, result_out[side][t], count(h, 16), passed_pool)
                    if t == 0:
                        col = slot_i[:, :, b * TT:(b + 1) * TT] if isinstance(b, int) else \
                            slot_i[:, :, bass.ds(b * TT, TT)]
                        nc.gpsimd.tensor_copy(ridx[:, side, :, :], col).then_inc(ridx_done, 1)
                        wait_apart(pool, ridx_done, count(b, 1, 1), passed_pool)
                    for k, dst in enumerate((rows0, rows1)):
                        nc.gpsimd.indirect_dma_start(
                            out=dst[:, side, t, :], out_offset=None, in_=y_d[:, :],
                            in_offset=bass.IndirectOffsetOnAxis(ap=ridx[:, side, k, t:t + 1], axis=0))\
                            .then_inc(pair_in[side][t], 16)

            def gate_rows(b, side, h):
                for t in range(1, TT, 2):
                    wait(pool, pair_added, count(b, TT, t + 1))
                    if t == 1:
                        wait(pool, gb2_in[side], count(h, 16, 16))
                    nc.gpsimd.tensor_tensor(rows1[:, side, t, :], rows1[:, side, t, :], gb2[:, side, :], ALU.mult)\
                        .then_inc(gated_p, 1)

            fetch(0, 0, 0)
            fetch(1, 1, 0)
            gate_rows(0, 0, 0)
            with pool.Fori(1, NB // 2) as reg:
                fetch(2 * reg, 0, reg)
                gate_rows(2 * reg - 1, 1, reg - 1)
                fetch(2 * reg + 1, 1, reg)
                gate_rows(2 * reg, 0, reg)
            gate_rows(NB - 1, 1, NB // 2 - 1)

        @block.scalar
        def _(act):
            act.wait_ge(const_in, 64)
            nc.scalar.activation(scT[:, :, :], scT[:, :, :], ACT.Silu).then_inc(silu_c_ready, 1)

            def weight_high(i):
                c = CHUNKS.index(("w", i))
                act.wait_ge(chunk_in[c % 2], 16 * (c // 2 + 1))
                dst = wqkv_hi[:, :, i * D:(i + 1) * D] if i < 3 else wout_hi[:, :, :]
                nc.scalar.copy(dst, stage[c % 2]).then_inc(w_hi_done, 1)

            def ht_high(bank, uses, k, hT_read):
                wait(act, dense_free[bank], uses + 1)
                if k == 0 and hT_read is not None:
                    wait(act, long_ready, hT_read)
                nc.scalar.copy(hT_hi[:, k, :], ht_full[:, :]).then_inc(ht_hi_done, 1)

            def half_high(b, kind, i):
                which, done = (0, q_stacked) if kind == "q" else (1, k_stacked)
                if b is None:
                    bank, n, _ = place[(-1, kind, i)]
                    group = i
                else:
                    bank, n, _ = b.dense(kind, i)
                    group = b.lin(NG, i if i > 1 else i + NG)
                wait(act, long_ready, n + 1)
                wait(act, done, group * 256)
                nc.scalar.activation(half_hi[:, which, :], ps[:, D_BANK + bank, :], ACT.Copy,
                                     scale=SCALE if kind == "q" else 1.0).then_inc(half_hi_done, 1)

            for i in range(3):
                weight_high(i)
            for k in range(KT):
                ht_high(*place[(-1, "ht", k)][::2], k, None)
            half_high(None, "q", 0)
            half_high(None, "k", 0)

            def copy_values(b, i):
                bank, n, _ = place[(-1, "v", i)] if b is None else b.dense("v", i)
                wait(act, long_ready, n + 1)
                if b is not None:
                    wait(act, av_done, b.lin(U, 0))
                    if b.first and i == 0:
                        act.wait_ge(row_out, 16 * NMOD)
                nc.scalar.copy(values(0 if b is None else 1 - b.side, i),
                               ps[:, D_BANK + bank, :].rearrange("p (h c) -> p h c", c=HD))\
                    .then_inc(dense_free[bank], 1)

            for i in range(TT):
                copy_values(None, i)
            half_high(None, "q", 1)
            half_high(None, "k", 1)
            weight_high(3)
            nc.scalar.copy(wr_hi[:, :, :], wr_raw[:, :, :]).then_inc(w_hi_done, 1)

            def body(b):
                for u in range(TAIL_END if b.after_last else U):
                    for kind, i in b.work(u, 1):
                        bank, n, uses = b.dense(kind, i)
                        if kind == "ot":
                            g, t = i // TT % NG, i % TT
                            wait(act, short_ready, n + 1)
                            if 0 <= i < TT and not b.first:
                                wait(act, long_ready, b.dense("out", i)[1] + 1)
                            nc.scalar.copy(outT_hi[:, g, t * P:(t + 1) * P], ps[:, D_BANK + bank, 0:P])\
                                .then_inc(out_hi_done, 1)
                        if kind == "v":
                            copy_values(b, i)
                        if kind in "qk":
                            half_high(b, kind, i)
                        if kind == "tr":
                            wait(act, short_ready, n + 1)
                            wait(act, h2T_out, b.lin(16 * TT, 16 * (i - TT)))
                            wait(act, tr_lo_done, b.lin(TT, i - TT))
                            if i == 0:
                                wait(act, ht_lo_done, b.lin(KT, 0 if b.after_last else KT))
                            if i == 2 and b.has("ht", 0) and not b.after_last:
                                wait(act, ht_lo_done, b.lin(KT, 2 * KT))
                            nc.scalar.copy(h2T[:, :, :], ps[:, D_BANK + bank, :].rearrange("p (k n) -> p k n", k=KT))
                            if i:
                                wait(act, short_ready, b.dense("route", i - 1)[1] + 1)
                            elif b.reg is not None or b.at > 1:
                                wait(act, short_ready, b.dense("route", TT - 1, 1)[1] + 1)
                            nc.scalar.copy(h2T_hi[:, :, :], ps[:, D_BANK + bank, :].rearrange("p (k n) -> p k n", k=KT))\
                                .then_inc(dense_free[bank], 1)
                    if not b.after_last:
                        wait(act, max_ready, b.lin(U, u + 1))
                        wait(act, pt_ready, b.lin(U, u - 1))
                        nc.scalar.activation(probs[:, u % 2, :], ps[:, S_BANK + u % 2, :], ACT.Exp,
                                             bias=neg_top[:, u % 4:u % 4 + 1], scale=1.0).then_inc(exp_done, 1)
                        if u % 2 == 1:
                            m = u // 2
                            wait(act, gap_ready, b.lin(U, u + 1))
                            wait(act, pair_done, b.lin(U // 2, m - 1))
                            at = slice(2 * (m % 2), 2 * (m % 2) + 2)
                            nc.scalar.activation(inv[:, at, :], gap[:, at, :], ACT.Exp).then_inc(inv_ready, 1)
                    for kind, i in b.work(u, 1):
                        bank, n, uses = b.dense(kind, i)
                        if kind == "ht":
                            ht_high(bank, uses, i, b.dense("k", NG - 1)[1] + 1)
                    if before(b, u, 1):
                        c = u - 1
                        wait(act, pt_ready, b.lin(U, c + 1))
                        wait(act, av_done, b.lin(U, c - 1))
                        nc.scalar.copy(probsT[:, c % 2, :, :],
                                       ps[:, PT_BANK, :].rearrange("p (k n) -> p k n", k=TT)).then_inc(pt_free, 1)

            batches(act, body)
            phase_over(act, 1)

            act.wait_ge(s_w_in, 48)
            nc.scalar.copy(sgu_hi[:, :, :], sgu_raw).then_inc(s_w_hi, 1)
            nc.scalar.copy(swd_hi[:, :, :], swd_raw).then_inc(s_w_hi, 1)

            def shared_act(b):
                wait(act, s_in, count(b, 16, 16))
                wait(act, s_up_ready, count(b, 2 * MI))
                nc.scalar.copy(s_hi[:, :, :, :], s_raw[:, :, :, :]).then_inc(s_hi_done, 1)
                for m in range(MI):
                    wait(act, s_up_ready, count(b, 2 * MI, 2 * m + 1))
                    nc.scalar.activation(s_gate[:, m, :], ps[:, 2 * m, :], ACT.Silu).then_inc(s_gate_done, 1)
                for m in range(MI):
                    wait(act, s_act_done, count(b, MI, m + 1))
                    wait(act, s_down_ready, count(b, TT))
                    nc.scalar.copy(a_hi[:, m, :], s_act[:, m, :]).then_inc(a_hi_done, 1)

            shared_act(0)
            act.wait_ge(r_step, 2)
            nc.scalar.activation(prob, prob, ACT.Exp).then_inc(r_exp, 1)
            with act.Fori(1, NB) as reg:
                shared_act(reg)
            phase_over(act, 2)

            def store(c, i):
                wait(act, y_copied, count(i, RING, c + 1))
                dst = y_d[c * P:(c + 1) * P] if isinstance(i, int) and i == 0 else \
                    y_d[bass.ds(i * (RING * P) + c * P, P)] if not isinstance(i, int) else \
                    y_d[(i * RING + c) * P:(i * RING + c + 1) * P]
                act.dma_start(dst, yrow[:, c, :]).then_inc(y_out[c], 16)

            def routed_act(i):
                for c in range(RING):
                    wait(act, xt_ready, count(i, RING, c + 1))
                    wait(act, gu_ready, count(i, RING, c - 1))
                    nc.scalar.copy(xT[:, c % 2, :, :],
                                   ps[:, c % 2, :].rearrange("p (k n) -> p k n", k=KT)).then_inc(xt_copied, 1)
                    wait(act, gu_ready, count(i, RING, c + 1))
                    wait(act, inner_done, count(i, RING, c - 1))
                    nc.scalar.activation(gate[:, c % 2, :], ps[:, 2 + c % 2, 0:FI], ACT.Silu)\
                        .then_inc(gate_done, 1)
                    if c >= 2:
                        store(c - 2, i)
                    elif not isinstance(i, int):
                        store(c + 2, i - 1)

            routed_act(0)
            with act.Fori(1, NST // RING) as reg:
                routed_act(reg)
            store(2, NST // RING - 1)
            store(3, NST // RING - 1)
            for c in range(RING):
                act.wait_ge(y_out[c], 16 * NST // RING)
            phase_over(act, 3)

            def combine_act(b, side, h):
                for t in range(TT):
                    wait(act, pair_in[side][t], count(h, 32, 32))
                    w = wts[:, 0, b * TT + t:b * TT + t + 1] if isinstance(b, int) else wts[:, 0, bass.ds(b * TT + t, 1)]
                    nc.scalar.activation(rows0[:, side, t, :], rows0[:, side, t, :], ACT.Copy, scale=w)\
                        .then_inc(first_scaled, 1)

            each_pair(act, combine_act)

        @block.vector
        def _(dve):
            def weight_low(i):
                c = CHUNKS.index(("w", i))
                dve.wait_ge(w_hi_done, i + 1)
                hi, lo = ((w[:, :, i * D:(i + 1) * D] for w in (wqkv_hi, wqkv_lo)) if i < 3
                          else (wout_hi[:, :, :], wout_lo[:, :, :]))
                nc.vector.tensor_tensor(lo, stage[c % 2], hi, ALU.subtract).then_inc(w_lo_done, 1)

            def ln1_stats(need_x, t):
                wait(dve, x_in, need_x)
                nc.vector.bn_stats(stats1[:, t, :], xnat[:, t, :]).then_inc(ln1_step, 1)

            def ln1_mean(n9):
                wait_apart(dve, ln1_step, n9 + TT, passed_dve)
                for t in range(TT):
                    nc.vector.bn_aggr(mv1[:, t, :], stats1[:, t, :]).then_inc(ln1_step, 1)

            def normalize1(n, t):
                wait(dve, rstd1_step, n * 2)
                nc.vector.tensor_scalar(xnat[:, t, :], xnat[:, t, :], mv1[:, t, 0:1], rstd1[:, t:t + 1],
                                        ALU.subtract, ALU.mult).then_inc(xn_done, 1)

            def ht_whole(n, k, place_of, nb):
                bank, at, _ = place_of
                wait(dve, long_ready, at + 1)
                wait(dve, ht_lo_done, n)
                if isinstance(nb, int):
                    ca, sa = modT[:, 1, k, nb:nb + 1], modT[:, 0, k, nb:nb + 1]
                else:
                    ca, sa = modT[:, 1, k, bass.ds(nb, 1)], modT[:, 0, k, bass.ds(nb, 1)]
                nc.vector.tensor_scalar(ht_full[:, :], ps[:, D_BANK + bank, :], ca, sa, ALU.mult,
                                        ALU.add).then_inc(dense_free[bank], 1)

            def half_low(b, kind, i):
                which = 0 if kind == "q" else 1
                bank = (place[(-1, kind, i)] if b is None else b.dense(kind, i))[0]
                halves = 2 * i if b is None else b.lin(2 * NG, 2 * (i if i > 1 else i + NG))
                wait(dve, half_hi_done, halves + which + 1)
                nc.vector.scalar_tensor_tensor(half_lo[:, which, :], ps[:, D_BANK + bank, :],
                                               SCALE if kind == "q" else 1.0, half_hi[:, which, :],
                                               ALU.mult, ALU.subtract).then_inc(dense_free[bank], 1)

            bank, at, _ = place[(-1, "modT", 0)]
            dve.wait_ge(short_ready, at + 1)
            cols = ps[:, D_BANK + bank, 0:2 * KT * NB].rearrange("p (m k b) -> p m k b", m=2, k=KT)
            nc.vector.tensor_copy(modT[:, 0, :, :], cols[:, 0, :, :])
            nc.vector.tensor_scalar_add(modT[:, 1, :, :], cols[:, 1, :, :], 1.0).then_inc(dense_free[bank], 1)
            dve.wait_ge(dense_free[bank], 1)
            for t in range(TT):
                ln1_stats(16, t)
            ln1_mean(0)
            for t in range(TT):
                normalize1(1, t)
            for i in range(2):
                weight_low(i)
            for k in range(KT):
                ht_whole(k, k, place[(-1, "ht", k)], 0)
            weight_low(2)
            half_low(None, "q", 0)
            half_low(None, "k", 0)
            dve.wait_ge(const_in, 64)
            for m in range(4):
                if m == 2:
                    half_low(None, "q", 1)
                    half_low(None, "k", 1)
                bank, at, uses = place[(-1, "mod", m)]
                dve.wait_ge(long_ready, at + 1)
                got = ps[0:NB, D_BANK + bank, :]
                if m in (0, 3):
                    nc.vector.tensor_scalar(V[0:NB, 1, 0, 0:D], got, 0.0, 2.0, ALU.is_ge, ALU.mult)
                    nc.vector.tensor_scalar(V[0:NB, 1, 1, 0:D], got, -1.0, None, ALU.mult).then_inc(gate_step, 1)
                    dve.wait_ge(gate_step, 3 * (m // 3) + 1)
                    nc.vector.tensor_tensor(V[0:NB, 1, 1, 0:D], got, V[0:NB, 1, 1, 0:D], ALU.max)\
                        .then_inc(dense_free[bank], 1)
                    dve.wait_ge(dense_free[bank], uses + 1)
                    nc.vector.tensor_scalar_max(V[0:NB, 1, 1, 0:D], V[0:NB, 1, 1, 0:D], 0.25).then_inc(gate_step, 1)
                    dve.wait_ge(gate_step, 3 * (m // 3) + 2)
                    nc.vector.tensor_scalar_add(V[0:NB, 1, 0, 0:D], V[0:NB, 1, 0, 0:D], -1.0).then_inc(gate_step, 1)
                    dve.wait_ge(gate_step, 3 * (m // 3) + 3)
                    nc.vector.tensor_tensor(bc[0:NB, m, :], V[0:NB, 1, 0, 0:D], V[0:NB, 1, 1, 0:D],
                                            ALU.mult).then_inc(row_step, 1)
                    if m == 0:
                        dve.wait_ge(row_step, 1)
                        nc.vector.tensor_tensor(V[0:NB, 1, 2, 0:D], bc[0:NB, 0, :], V[0:NB, 1, 3, 0:D],
                                                ALU.mult).then_inc(row_step, 1)
                else:
                    nc.vector.tensor_scalar_add(bc[0:NB, m, :], got, 1.0 if m == 1 else 0.0)\
                        .then_inc(row_step, 1)
                    dve.wait_ge(row_step, m + 2)
                    dve.sem_inc(dense_free[bank], 1)
            weight_low(3)
            dve.wait_ge(w_hi_done, 5)
            nc.vector.tensor_tensor(wr_lo[:, :, :], wr_raw[:, :, :], wr_hi[:, :, :],
                                    ALU.subtract).then_inc(w_lo_done, 1)

            def body(b):
                for u in range(TAIL_END if b.after_last else U):
                    if not b.after_last:
                        wait(dve, scores_ready, b.lin(U, u + 1))
                        wait(dve, exp_done, b.lin(U, u - 3))
                        nc.vector.reduce_max(neg_max[:, u % 4, :],
                                             ps[:, S_BANK + u % 2, :].rearrange("p (k n) -> p k n", k=TT), AX.X,
                                             negate=True).then_inc(block_max_done, 1)
                        wait(dve, block_max_done, b.lin(U, u + 1))
                        nc.vector.tensor_reduce(neg_top[:, u % 4:u % 4 + 1], neg_max[:, u % 4, :], AX.X,
                                                ALU.min).then_inc(max_ready, 1)
                        wait(dve, max_ready, b.lin(U, u + 1))
                        wait(dve, inv_ready, b.lin(U // 2, u // 2 - 1))
                        nc.vector.tensor_scalar(gap[:, u % 4, :], neg_max[:, u % 4, :],
                                                neg_top[:, u % 4:u % 4 + 1], GAP_MAX, ALU.subtract,
                                                ALU.min).then_inc(gap_ready, 1)
                    for kind, i in b.work(u, 1):
                        bank, n, uses = b.dense(kind, i)
                        if kind in "qk":
                            half_low(b, kind, i)
                        if kind == "ot":
                            g, t = i // TT % NG, i % TT
                            wait(dve, out_hi_done, b.lin(NG * TT, i + 1))
                            nc.vector.tensor_tensor(outT_lo[:, g, t * P:(t + 1) * P], ps[:, D_BANK + bank, 0:P],
                                                    outT_hi[:, g, t * P:(t + 1) * P],
                                                    ALU.subtract).then_inc(dense_free[bank], 1)
                        if kind == "out":
                            wait(dve, long_ready, n + 1)
                            if i == 0:
                                wait(dve, bc_in, b.lin(64, 0))
                            wait(dve, x1_out[i % 2], b.lin(16 * TT // 2, 16 * (i // 2) - 16 * TT // 2))
                            wait(dve, h2_normal, b.lin(TT, max(i - 1, 0) - TT))
                            nc.vector.tensor_tensor(post[:, 2 + i % 2, :], ps[:, D_BANK + bank, :], bc[:, 0, :],
                                                    ALU.mult).then_inc(dense_free[bank], 1)
                        if kind == "route":
                            wait(dve, short_ready, n + 1)
                            dst = logits[:, TT * (b.at - 1) + i, :] if b.reg is None else \
                                logits[:, bass.ds(b.lin(TT, i - TT), 1), :].rearrange("p a e -> p (a e)")
                            nc.vector.tensor_tensor(dst, ps[:, D_BANK + bank, 0:NE], rbias[:, :],
                                                    ALU.add).then_inc(dense_free[bank], 1)
                        if kind == "ht":
                            if i == 0:
                                wait(dve, h2T_out, b.lin(16 * TT, -32))
                                wait(dve, tr_lo_done, b.lin(TT, -2))
                            ht_whole(b.lin(KT, KT + i), i, b.dense(kind, i), b.lin(1, 1))
                    if u % 2 == 0 and before(b, u, 4):
                        m = (u - 4) // 2
                        n = b.lin(3 * U // 2, 3 * m)
                        got = ps[:, AV_BANK + m % 2, 0:2 * TT * VW].rearrange("p (a k c) -> p a k c", a=2, k=TT)
                        sums = got[:, :, :, HD]
                        heads = slice(2 * (m % 2), 2 * (m % 2) + 2)
                        wait(dve, inv_ready, b.lin(U // 2, m + 1))
                        wait(dve, av_done, b.lin(U, 2 * m + 2))
                        nc.vector.tensor_tensor(weighed[:, :, :], sums, inv[:, heads, :], ALU.mult)
                        nc.vector.reduce_sum(total[:, :], sums, AX.X).then_inc(factor_step, 1)
                        wait(dve, factor_step, n + 1)
                        nc.vector.reciprocal(total[:, :], total[:, :]).then_inc(factor_step, 1)
                        wait(dve, factor_step, n + 2)
                        nc.vector.tensor_tensor(factor[:, :, :], weighed[:, :, :],
                                                total[:, :].unsqueeze(2).broadcast_to([P, 2, TT]),
                                                ALU.mult).then_inc(factor_step, 1)
                        wait(dve, factor_step, n + 3)
                        nc.vector.tensor_tensor(
                            tile_rows[:, m // 2 % 2, :, heads, :].rearrange("p k a c -> p a k c"),
                            got[:, :, :, 0:HD], factor[:, :, :].unsqueeze(3).broadcast_to([P, 2, TT, HD]),
                            ALU.mult).then_inc(pair_done, 1)
                    for kind, i in b.work(u, 3):
                        if kind == "out":
                            n2 = b.lin(2 * TT, 2 * (i - TT))
                            wait(dve, x1_done, b.lin(TT, i - TT + 1))
                            nc.vector.bn_stats(stats2[:, i % 2, :], post[:, 2 + i % 2, :]).then_inc(ln2_step, 1)
                            wait_apart(dve, ln2_step, n2 + 1, passed_dve)
                            nc.vector.bn_aggr(mv2[:, i % 2, :], stats2[:, i % 2, :]).then_inc(ln2_step, 1)
                    for kind, i in b.work(u, 4):
                        if kind == "out":
                            wait(dve, rstd2_step, b.lin(2 * TT, 2 * (i + 1 - TT)))
                            if i == 0:
                                wait(dve, h2_out, b.lin(16 * TT, -16 * TT))
                                wait(dve, tr_lo_done, b.lin(TT, -TT))
                            nc.vector.tensor_scalar(h2[:, i, :], post[:, 2 + i % 2, :], mv2[:, i % 2, 0:1],
                                                    rstd2[:, i % 2:i % 2 + 1], ALU.subtract,
                                                    ALU.mult).then_inc(h2_normal, 1)
                    if not b.after_last and b.has("ht", 0):
                        n9 = b.lin(2 * TT, 2 * TT)
                        if 16 <= u < 16 + TT:
                            ln1_stats(b.lin(16, 32), u - 16)
                        if u == 22:
                            ln1_mean(n9)
                        if 24 <= u < 24 + TT:
                            normalize1(b.lin(1, 2), u - 24)

            batches(dve, body)
            phase_over(dve, 1)

            for n, (lo, raw, hi) in enumerate(((sgu_lo, sgu_raw, sgu_hi), (swd_lo, swd_raw, swd_hi))):
                dve.wait_ge(s_w_hi, n + 1)
                nc.vector.tensor_tensor(lo[:, :, :], raw, hi[:, :, :], ALU.subtract).then_inc(s_w_lo, 1)

            def half_low_rows(n):
                wait(dve, s_hi_done, n)
                nc.vector.tensor_tensor(s_lo[:, 0:TT // 2, :, :], s_raw[:, 0:TT // 2, :, :],
                                        s_hi[:, 0:TT // 2, :, :], ALU.subtract).then_inc(s_lo_v, 1)

            def shared_dve(b, last=False):
                for m in range(MI):
                    wait(dve, s_gate_done, count(b, MI, m + 1))
                    wait(dve, s_up_ready, count(b, 2 * MI, 2 * m + 2))
                    wait(dve, a_lo_done, count(b, MI))
                    nc.vector.tensor_tensor(s_act[:, m, :], s_gate[:, m, :], ps[:, 2 * m + 1, :],
                                            ALU.mult).then_inc(s_act_done, 1)
                if not last:
                    half_low_rows(count(b, 1, 2))
                wait(dve, s_gb_in, count(b, 16, 16))
                for t in range(TT):
                    wait(dve, s_down_ready, count(b, TT, t + 1))
                    wait(dve, base_done, count(b, TT, t - 1))
                    nc.vector.tensor_tensor(scaled[:, t % 2, :], ps[:, 4 + t, :], gbrow[:, :],
                                            ALU.mult).then_inc(scaled_done, 1)

            half_low_rows(1)
            shared_dve(0, last=True)

            step = [0]

            def then(ins):
                step[0] += 1
                ins.then_inc(r_step, 1)
                dve.wait_ge(r_step, step[0])

            def te(v):
                return v.rearrange("p (t e) -> p t e", e=NE)

            def over_e(v):
                return v.unsqueeze(2).broadcast_to([P, NT, NE])

            L = logits[:, :, :]
            experts = iota_e.unsqueeze(1).broadcast_to([P, NT, NE])
            then(nc.vector.reduce_max(row_max, L, AX.X))
            then(nc.vector.tensor_tensor(te(prob), L, over_e(row_max), ALU.subtract))
            dve.wait_ge(r_exp, 1)
            then(nc.vector.reduce_sum(row_sum, te(prob), AX.X))
            then(nc.vector.reciprocal(row_sum, row_sum))
            then(nc.vector.tensor_tensor(te(prob), te(prob), over_e(row_sum), ALU.mult))
            dve.wait_ge(r_const, 8)
            left = prob
            for k in range(2):
                then(nc.vector.reduce_max(top[k], te(left), AX.X))
                then(nc.vector.tensor_tensor(te(eq), te(left), over_e(top[k]), ALU.is_equal))
                then(nc.vector.scalar_tensor_tensor(te(order), te(eq), -float(NE), experts, ALU.mult, ALU.add))
                then(nc.vector.tensor_reduce(first, te(order), AX.X, ALU.min))
                then(nc.vector.tensor_tensor(te(oh[k]), te(order), over_e(first), ALU.is_equal))
                if k == 0:
                    then(nc.vector.scalar_tensor_tensor(slot_of, oh[0], -2.0, prob, ALU.mult, ALU.add))
                    left = slot_of
            nc.vector.tensor_tensor(mask[:, :], oh[0], oh[1], ALU.add).then_inc(mask_ready, 1)
            half_low_rows(2)
            then(nc.vector.tensor_tensor(den, top[0], top[1], ALU.add))
            then(nc.vector.tensor_scalar_add(den, den, 1e-9))
            then(nc.vector.reciprocal(den, den))
            for k in range(2):
                then(nc.vector.tensor_tensor(wts[:, k, :], top[k], den, ALU.mult))
            dve.wait_ge(rank_ready, 1)
            then(nc.vector.tensor_copy(tot_e.rearrange("p (e t) -> p e t", e=NE),
                                       ps[:, 1, :].rearrange("p (t e) -> p e t", e=NE)))
            then(nc.vector.tensor_tensor_scan(run, ones_te, tot_e, 0.0, ALU.mult, ALU.add))
            ends = run.rearrange("p (e t) -> p e t", e=NE)[:, :, NT - 1]
            then(nc.vector.memset(cum_prev, 0.0))
            then(nc.vector.tensor_copy(cum_prev[:, 1:NE], ends[:, 0:NE - 1]))
            then(nc.vector.tensor_tensor(cnt, ends, cum_prev, ALU.subtract))
            then(nc.vector.tensor_scalar_add(tiles_i, cnt, float(P - 1)))
            then(nc.vector.tensor_scalar(tiles_i, tiles_i, 7, None, ALU.logical_shift_right))
            then(nc.vector.tensor_copy(tiles, tiles_i))
            then(nc.vector.tensor_tensor_scan(tiles_cum, ones_te[:, 0:NE], tiles, 0.0, ALU.mult, ALU.add))
            then(nc.vector.tensor_tensor(offset, tiles_cum, tiles, ALU.subtract))
            then(nc.vector.scalar_tensor_tensor(offset, offset, float(P), cum_prev, ALU.mult, ALU.subtract))
            then(nc.vector.tensor_tensor(run, run, tot_e, ALU.subtract))
            then(nc.vector.tensor_tensor(run.rearrange("p (e t) -> p e t", e=NE),
                                         run.rearrange("p (e t) -> p e t", e=NE),
                                         offset.unsqueeze(2).broadcast_to([P, NE, NT]), ALU.add))
            then(nc.vector.tensor_tensor(te(slot_of), te(ps[:, 0, :]),
                                         run.rearrange("p (e t) -> p t e", e=NE), ALU.add))
            dve.sem_inc(slots_ready, 1)
            for k in range(2):
                then(nc.vector.tensor_tensor(eq, slot_of, oh[k], ALU.mult))
                then(nc.vector.reduce_sum(slots[:, k * NT:(k + 1) * NT], te(eq), AX.X))
            then(nc.vector.tensor_copy(slot_i[:, :, :].rearrange("p k t -> p (k t)"), slots))
            si = slot_i[:, :, :].rearrange("p k t -> p (k t)")
            then(nc.vector.tensor_scalar(tmp_i, si, 7, None, ALU.logical_shift_right))
            then(nc.vector.tensor_scalar(tmp2_i, si, P - 1, None, ALU.bitwise_and))
            then(nc.vector.tensor_copy(slots_hi, tmp_i))
            then(nc.vector.tensor_copy(slots_lo, tmp2_i))
            big = wslots[:, 2 * WLEN:2 * WLEN + NST * NE].rearrange("p (t e) -> p t e", e=NE)
            then(nc.vector.tensor_tensor(big, iota_t.unsqueeze(2).broadcast_to([P, NST, NE]),
                                         tiles_cum.unsqueeze(1).broadcast_to([P, NST, NE]), ALU.is_ge))
            then(nc.vector.reduce_sum(e_tab, big, AX.X))
            then(nc.vector.tensor_scalar_min(e_tab, e_tab, float(NE - 1)))
            then(nc.vector.tensor_copy(e_tab_i, e_tab))
            then(nc.vector.tensor_scalar_add(need_i[0:1, :], e_tab[0:1, :], 1.0))
            then(nc.vector.tensor_scalar(e_tab_i, e_tab_i, WSLOTS - 1, None, ALU.bitwise_and))
            then(nc.vector.tensor_copy(e_tab, e_tab_i))
            then(nc.vector.tensor_scalar(woff_i[0:1, :], e_tab[0:1, :], float(WLEN), None, ALU.mult))
            then(nc.vector.tensor_scalar_add(freed_i[0:1, :], tiles_cum[0:1, :], 1.0))

            with dve.Fori(1, NB - 1) as reg:
                shared_dve(reg)
            shared_dve(NB - 1, last=True)

            for g in range(2 * NT // HOTS):
                n, m = g * HOTS, g * HOTS % NT
                if g >= 2:
                    dve.wait_ge(hot_used, (g - 1) * HOTS)
                nc.vector.tensor_tensor(hot_lo[:, g % 2, :, :], iota_p[:, :].unsqueeze(1).broadcast_to([P, HOTS, P]),
                                        slots_lo[:, n:n + HOTS].unsqueeze(2).broadcast_to([P, HOTS, P]),
                                        ALU.is_equal)
                if g:
                    dve.wait_ge(hot_done, g)
                nc.vector.tensor_tensor(hot_at[:, :, :], iota_t.unsqueeze(1).broadcast_to([P, HOTS, NST]),
                                        slots_hi[:, n:n + HOTS].unsqueeze(2).broadcast_to([P, HOTS, NST]),
                                        ALU.is_equal).then_inc(hot_step, 1)
                dve.wait_ge(hot_step, g + 1)
                nc.vector.tensor_tensor(hot_hi[:, g % 2, :, :], hot_at[:, :, :],
                                        tokid[:, m:m + HOTS].unsqueeze(2).broadcast_to([P, HOTS, NST]),
                                        ALU.mult).then_inc(hot_done, 1)
            dve.wait_ge(hot_used, 2 * NT)
            nc.vector.tensor_copy(gather_i[:, :], ps[:, 0, 0:NST])
            phase_over(dve, 2)

            def routed_dve(i):
                for c in range(RING):
                    wait(dve, gate_done, count(i, RING, c + 1))
                    wait(dve, innerT_ready, count(i, RING, c - 1))
                    nc.vector.tensor_tensor(inner[:, c % 2, :], gate[:, c % 2, :], ps[:, 2 + c % 2, FI:],
                                            ALU.mult).then_inc(inner_done, 1)
                    if c or not isinstance(i, int):
                        y_copy(c - 1 if c else RING - 1, i if c else i - 1)
                    wait(dve, innerT_ready, count(i, RING, c + 1))
                    wait(dve, y_ready, count(i, RING, c))
                    nc.vector.tensor_copy(innerT[:, c % 2, :, :],
                                          ps[:, 4 + c % 2, 0:MI * P].rearrange("p (m n) -> p m n", m=MI))\
                        .then_inc(innerT_copied, 1)

            def y_copy(c, i):
                wait(dve, y_ready, count(i, RING, c + 2))
                wait(dve, y_out[c], count(i, 16))
                nc.vector.tensor_copy(yrow[:, c, :], ps[:, 6 + c % 2, :]).then_inc(y_copied, 1)

            routed_dve(0)
            with dve.Fori(1, NST // RING) as reg:
                routed_dve(reg)
            y_copy(RING - 1, NST // RING - 1)
            phase_over(dve, 3)

            def combine_dve(b, side, h):
                for t in range(TT):
                    wait(dve, first_scaled, count(b, TT, t + 1))
                    w = wts[:, 1, b * TT + t:b * TT + t + 1] if isinstance(b, int) else wts[:, 1, bass.ds(b * TT + t, 1)]
                    nc.vector.scalar_tensor_tensor(rows1[:, side, t, :], rows1[:, side, t, :], w, rows0[:, side, t, :],
                                                   ALU.mult, ALU.add).then_inc(pair_added, 1)
                    if t % 2 == 0:
                        wait(dve, pair_added, count(b, TT, t + 1))
                        if t == 0:
                            wait(dve, gb2_in[side], count(h, 16, 16))
                        nc.vector.tensor_tensor(rows1[:, side, t, :], rows1[:, side, t, :], gb2[:, side, :], ALU.mult)\
                            .then_inc(gated_v, 1)
                for t in range(TT):
                    wait(dve, gated_p if t % 2 else gated_v, count(b, TT // 2, t // 2 + 1))
                    row = base[:, b * TT + t, :] if isinstance(b, int) else \
                        base[:, bass.ds(b * TT + t, 1), :].rearrange("p a d -> p (a d)")
                    nc.vector.tensor_tensor(rows1[:, side, t, :], rows1[:, side, t, :], row, ALU.add)\
                        .then_inc(result_done, 1)

            each_pair(dve, combine_dve)

        @block.tensor
        def _(pe):
            def three(out_ap, lhs_hi, lhs_lo, rhs_hi, rhs_lo, start, stop):
                nc.tensor.matmul(out_ap, lhs_hi, rhs_hi, start=start, stop=False)
                nc.tensor.matmul(out_ap, lhs_lo, rhs_hi, start=False, stop=False)
                return nc.tensor.matmul(out_ap, lhs_hi, rhs_lo, start=False, stop=stop)

            def dense(b, kind, i, ks=range(KT)):
                bank, n, uses = place[(-1, kind, i)] if b is None else b.dense(kind, i)
                if 0 in ks:
                    wait(pe, dense_free[bank], uses)
                to = ps[:, D_BANK + bank, :]
                if kind == "modT":
                    pe.wait_ge(silu_c_ready, 1)
                    for m in range(2):
                        pe.wait_ge(chunk_in[m], 16)
                        for kt in range(KT):
                            for k in range(KT):
                                last = nc.tensor.matmul(to[:, (m * KT + kt) * NB:(m * KT + kt + 1) * NB],
                                                        stage[m][:, k, kt * P:(kt + 1) * P], scT[:, k, :],
                                                        start=k == 0, stop=k == KT - 1)
                elif kind == "mod":
                    c = CHUNKS.index((kind, i))
                    pe.wait_ge(chunk_in[c % 2], 16 * (c // 2 + 1))
                    for k in range(KT):
                        last = nc.tensor.matmul(to[0:NB, :], scT[:, k, :], stage[c % 2][:, k, :],
                                                start=k == 0, stop=k == KT - 1)
                elif kind == "ht":
                    if i == 0:
                        pe.wait_ge(identity_ready, 2)
                        wait(pe, xn_done, TT if b is None else b.lin(TT, 2 * TT))
                    for t in range(TT):
                        last = nc.tensor.transpose(to[:, t * P:(t + 1) * P], xnat[:, t, i * P:(i + 1) * P],
                                                   ident[:, :])
                elif kind in "qk":
                    col = i * P + (0 if kind == "q" else D)
                    if b is None and i == 0:
                        pe.wait_ge(ht_lo_done, KT)
                        pe.wait_ge(w_lo_done, 1 if kind == "q" else 2)
                    for k in ks:
                        last = three(to, wqkv_hi[:, k, col:col + P], wqkv_lo[:, k, col:col + P],
                                     hT_hi[:, k, :], hT_lo[:, k, :], k == 0, k == KT - 1)
                elif kind == "v":
                    if b is None and i == 0:
                        pe.wait_ge(w_lo_done, 3)
                    at = slice(i * P, (i + 1) * P)
                    for k in ks:
                        if b is not None and i == 0:
                            wait(pe, ht_lo_done, b.lin(KT, KT + k + 1))
                        last = three(to, hT_hi[:, k, at], hT_lo[:, k, at],
                                     wqkv_hi[:, k, 2 * D:], wqkv_lo[:, k, 2 * D:], k == 0, k == KT - 1)
                elif kind == "out":
                    at = slice(i * P, (i + 1) * P)
                    for k in ks:
                        if i == 0 and k in (0, KT - 1):
                            slot, _, before_ot = b.dense("ot", 11, 1) if k == 0 else b.dense("ot", -1)
                            wait(pe, dense_free[slot], before_ot + 1)
                            pe.wait_ge(w_lo_done, 5)
                        last = three(to, outT_hi[:, k, at], outT_lo[:, k, at],
                                     wout_hi[:, k, :], wout_lo[:, k, :], k == 0, k == KT - 1)
                elif kind == "ot":
                    wait(pe, tile_step, b.lin(2 * NG * TT, 2 * (i + 1)))
                    last = nc.tensor.transpose(to[:, 0:P], tile_rows[:, i % 2, 0, :, :].rearrange("p j c -> p (j c)"),
                                               ident[:, :])
                elif kind == "tr":
                    wait(pe, h2_step, b.lin(2 * TT, 2 * (i + 1 - TT)))
                    for k in range(KT):
                        last = nc.tensor.transpose(to[:, k * P:(k + 1) * P], h2[:, i, k * P:(k + 1) * P],
                                                   ident[:, :])
                elif kind == "route":
                    wait(pe, tr_lo_done, b.lin(TT, i + 1 - TT))
                    for k in range(KT):
                        last = three(to[:, 0:NE], h2T_hi[:, k, :], h2T_lo[:, k, :],
                                     wr_hi[:, k, :], wr_lo[:, k, :], k == 0, k == KT - 1)
                if KT - 1 in ks:
                    last.then_inc(ready(kind), 1)

            for kind, i in PRO:
                dense(None, kind, i)

            def body(b):
                for u in range(TAIL_END if b.after_last else U):
                    g, t, j = u // UG, u // HG % TT, u % HG
                    if not b.after_last:
                        if u % UG == 0:
                            wait(pe, q_stacked, b.lin(256 * NG, 256 * (g + 1)))
                            wait(pe, k_stacked, b.lin(256 * NG, 256 * (g + 1)))
                        wait(pe, exp_done, b.lin(U, u - 1))
                        nc.tensor.matmul(ps[:, S_BANK + u % 2, :], qstack[:, g % 2, j, t * P:(t + 1) * P],
                                         kstack[:, g % 2, j, :], start=True, stop=True)\
                            .then_inc(scores_ready, 1)
                    for kind, i, ks in b.parts(u):
                        dense(b, kind, i, ks)
                    if before(b, u, 1):
                        c = u - 1
                        wait(pe, exp_done, b.lin(U, c + 1))
                        wait(pe, pt_free, b.lin(U, c))
                        for k in range(TT):
                            last = nc.tensor.transpose(ps[:, PT_BANK, k * P:(k + 1) * P],
                                                       probs[:, c % 2, k * P:(k + 1) * P], ident[:, :])
                        last.then_inc(pt_ready, 1)
                    if before(b, u, 2):
                        c = u - 2
                        if c == 0:
                            bank, _, uses = b.dense("v", TT - 1, 1)
                            wait(pe, dense_free[bank], uses + 1)
                            if b.reg is None and b.at < 2:
                                pe.wait_ge(ones_ready, b.at + 1)
                        if c % 2 == 0:
                            wait(pe, pair_done, b.lin(U // 2, c // 2 - 1))
                        wait(pe, pt_free, b.lin(U, c + 1))
                        side = b.side if c >= 0 else 1 - b.side
                        head = c // UG % NG * HG + c % HG
                        for k in range(TT):
                            to = (c % 2 * TT + k) * VW
                            last = nc.tensor.matmul(ps[:, AV_BANK + c // 2 % 2, to:to + VW],
                                                    probsT[:, c % 2, k, :],
                                                    V[:, side, k, head * VW:(head + 1) * VW],
                                                    start=True, stop=True)
                        last.then_inc(av_done, 1)

            batches(pe, body)
            phase_over(pe, 1)

            def shared_pe(b):
                wait(pe, s_lo_v, count(b, 1, 1))
                wait(pe, s_lo_p, count(b, 1, 1))
                if isinstance(b, int):
                    pe.wait_ge(s_w_lo, 2)
                for m in range(MI):
                    wait(pe, s_act_done, count(b, MI))
                    for n in range(2):
                        col = slice(n * FI + m * P, n * FI + (m + 1) * P)
                        for k in range(KT):
                            last = three(ps[:, 2 * m + n, :], sgu_hi[:, k, col], sgu_lo[:, k, col],
                                         s_hi[:, :, k, :], s_lo[:, :, k, :], k == 0, k == KT - 1)
                        last.then_inc(s_up_ready, 1)
                wait(pe, a_lo_done, count(b, MI, MI))
                for t in range(TT):
                    wait(pe, scaled_done, count(b, TT, t + 1 - TT))
                    for m in range(MI):
                        last = three(ps[:, 4 + t, :], a_hi[:, m, t * P:(t + 1) * P], a_lo[:, m, t * P:(t + 1) * P],
                                     swd_hi[:, m, :], swd_lo[:, m, :], m == 0, m == MI - 1)
                    last.then_inc(s_down_ready, 1)

            shared_pe(0)
            pe.wait_ge(mask_ready, 1)
            nc.tensor.matmul(ps[:, 0, :], tri[:, :], mask[:, :], start=True, stop=True)
            nc.tensor.matmul(ps[:, 1, :], ones_b[:, :], mask[:, :], start=True, stop=True).then_inc(rank_ready, 1)
            pe.wait_ge(slots_ready, 1)
            with pe.Fori(1, NB) as reg:
                shared_pe(reg)
            pe.wait_ge(s_act_done, NB * MI)
            for n in range(2 * NT):
                pe.wait_ge(hot_done, n // HOTS + 1)
                nc.tensor.matmul(ps[:, 0, 0:NST], hot_lo[:, n // HOTS % 2, n % HOTS, :],
                                 hot_hi[:, n // HOTS % 2, n % HOTS, :],
                                 start=n == 0, stop=n == 2 * NT - 1).then_inc(hot_used, 1)
            phase_over(pe, 2)

            pe.sem_inc(y_ready, 1)

            def x_transposed(c, i):
                wait(pe, rows_in[c], count(i, 16, 16))
                wait(pe, xt_copied, count(i, RING, c - 1))
                for k in range(KT):
                    last = nc.tensor.transpose(ps[:, c % 2, k * P:(k + 1) * P], xg[:, c, k * P:(k + 1) * P],
                                               ident[:, :])
                last.then_inc(xt_ready, 1)

            def weights(i, c):
                n = slice(c + RING * i, c + RING * i + 1) if isinstance(i, int) else bass.ds(i * RING + c, 1)
                return (pe.value_load(need_i[0:1, n], min_val=1, max_val=NE),
                        pe.value_load(woff_i[0:1, n], min_val=0, max_val=(WSLOTS - 1) * WLEN))

            def down(c, i, woff):
                wait(pe, innerT_copied, count(i, RING, c + 1))
                wait(pe, y_copied, count(i, RING, c - 1))
                for m in range(MI):
                    last = nc.tensor.matmul(ps[:, 6 + c % 2, :], innerT[:, c % 2, m, :],
                                            wslots[:, bass.ds(woff + (KT * 2 * FI + m * D), D)],
                                            start=m == 0, stop=m == MI - 1)
                last.then_inc(y_ready, 1)

            def routed_pe(i, last_one=False):
                need, woff = weights(i, 0)
                for c in range(RING):
                    if c + 1 < RING:
                        x_transposed(c + 1, i)
                    elif not last_one:
                        x_transposed(0, i + 1)
                    pe.wait_ge(weights_ready, need)
                    wait(pe, xt_copied, count(i, RING, c + 1))
                    wait(pe, inner_done, count(i, RING, c - 1))
                    for k in range(KT):
                        last = nc.tensor.matmul(ps[:, 2 + c % 2, :], xT[:, c % 2, k, :],
                                                wslots[:, bass.ds(woff + k * 2 * FI, 2 * FI)],
                                                start=k == 0, stop=k == KT - 1)
                    last.then_inc(gu_ready, 1)
                    if c:
                        down(c - 1, i, woff_before)
                    elif not (isinstance(i, int) and i == 0):
                        down(RING - 1, i - 1, weights(i - 1, RING - 1)[1])
                    woff_before = woff
                    if c + 1 < RING:
                        need, woff = weights(i, c + 1)
                    wait(pe, inner_done, count(i, RING, c + 1))
                    wait(pe, innerT_copied, count(i, RING, c - 1))
                    for m in range(MI):
                        last = nc.tensor.transpose(ps[:, 4 + c % 2, m * P:(m + 1) * P],
                                                   inner[:, c % 2, m * P:(m + 1) * P], ident[:, :])
                    last.then_inc(innerT_ready, 1)

            x_transposed(0, 0)
            routed_pe(0)
            with pe.Fori(1, NST // RING - 1) as reg:
                routed_pe(reg)
            routed_pe(NST // RING - 1, last_one=True)
            down(RING - 1, NST // RING - 1, weights(NST // RING - 1, RING - 1)[1])
            phase_over(pe, 3)


def kernel(**inputs):
    import numpy as np
    import concourse.bacc as bacc
    from concourse import mybir
    from concourse.bass_utils import run_bass_kernel_spmd

    def given(name):
        return np.asarray(inputs["L0_" + name])

    arrays = {
        "x": given("attn_x"), "wqkvT": given("attn_w_qkv").T, "woutT": given("attn_w_out").T,
        "b_out": given("attn_b_out"), "wrT": given("ffn_Wr").T, "r_bias": given("ffn_bias"),
        "Wg": given("ffn_Wg"), "Wu": given("ffn_Wu"), "Wd": given("ffn_Wd"),
        "sWg": given("ffn_sWg"), "sWu": given("ffn_sWu"), "sWd": given("ffn_sWd"),
        "cT": given("c").T, "wmod": given("wmod"),
    }
    arrays = {f"in_{name}_dram": np.ascontiguousarray(a) for name, a in arrays.items()}
    nc = bacc.Bacc("TRN2", target_bir_lowering=False, num_devices=1)
    args = [nc.dram_tensor(name, a.shape, mybir.dt.from_np(a.dtype), kind="ExternalInput").ap()
            for name, a in arrays.items()]
    x = arrays["in_x_dram"]
    out = nc.dram_tensor("out_0_dram", x.shape, mybir.dt.from_np(x.dtype), kind="ExternalOutput").ap()
    adaln_moe_block_kernel(nc, *args, out)
    r = run_bass_kernel_spmd(nc, [arrays], core_ids=[0])
    return r.results[0]["out_0_dram"]
```
